# Optimizing a Trainium2 kernel written in Bass

```python
import numpy as np
import jax
import jax.numpy as jnp

def _softmax(x, axis=-1):
    return jax.nn.softmax(x, axis=axis)

def _gelu(x):
    return jax.nn.gelu(x, approximate=True)

def _silu(x):
    return jax.nn.silu(x)

def _sigmoid(x):
    return jax.nn.sigmoid(x)

def _layernorm(x, axis=-1, eps=1e-05):
    m = jnp.mean(x, axis=axis, keepdims=True)
    v = jnp.var(x, axis=axis, keepdims=True)
    return (x - m) / jnp.sqrt(v + eps)

def _scatter_add(tgt, idx, src, axis=0):
    return tgt.at[idx].add(src)

def _segment_sum(src, seg, n):
    return jax.ops.segment_sum(src, seg, n)
kernel_name = 'mk_hybrid_d4_jaxref_r8_e2a317'

def setup_inputs(seed: int=0):
    np.random.seed(seed)
    _w = jnp.asarray

    def _L0_attn_a_setup():
        import jax, jax.numpy as jnp
        import numpy as np
        from jax import lax
        D_MODEL = 128
        D_INNER = 2 * D_MODEL
        D_STATE = 16
        D_CONV = 4
        DT_RANK = (D_MODEL + 15) // 16
        B, L = (4, 256)
        EPS = 1e-06

        def _rmsnorm(h, w):
            var = jnp.mean(h.astype(jnp.float32) ** 2, axis=-1, keepdims=True)
            return (w * (h * lax.rsqrt(var + EPS))).astype(h.dtype)

        def _mamba(x, in_proj_w, conv_w, conv_b, x_proj_w, dt_proj_w, dt_proj_b, A_log, D_skip, out_proj_w):
            xz = jnp.einsum('bld,ed->ble', x, in_proj_w)
            u, z = jnp.split(xz, 2, axis=-1)
            u_t = jnp.transpose(u, (0, 2, 1))
            conv = lax.conv_general_dilated(u_t, conv_w[:, None, :], (1,), [(D_CONV - 1, 0)], dimension_numbers=('NCH', 'OIH', 'NCH'), feature_group_count=D_INNER)
            u = jax.nn.silu(jnp.transpose(conv + conv_b[None, :, None], (0, 2, 1)))
            dbc = jnp.einsum('bld,ed->ble', u, x_proj_w)
            dt, Bm, Cm = jnp.split(dbc, [DT_RANK, DT_RANK + D_STATE], axis=-1)
            dt = jax.nn.softplus(jnp.einsum('blr,dr->bld', dt, dt_proj_w) + dt_proj_b)
            A = -jnp.exp(A_log)

            def step(s, inp):
                d, u_i, b_i, c_i = inp
                s = s * jnp.exp(d[..., None] * A) + (d * u_i)[..., None] * b_i[:, None, :]
                y = jnp.einsum('bdn,bn->bd', s, c_i)
                return (s, y)
            s0 = jnp.zeros((u.shape[0], D_INNER, D_STATE), u.dtype)
            inputs = (jnp.moveaxis(dt, 1, 0), jnp.moveaxis(u, 1, 0), jnp.moveaxis(Bm, 1, 0), jnp.moveaxis(Cm, 1, 0))
            _, ys = lax.scan(step, s0, inputs)
            y = jnp.moveaxis(ys, 0, 1) + u * D_skip
            y = y * jax.nn.silu(z)
            return jnp.einsum('ble,de->bld', y, out_proj_w)

        def _mlp(x, fc1_w, fc1_b, fc2_w, fc2_b, fc3_w, fc3_b):
            h = jax.nn.relu(jnp.einsum('bld,hd->blh', x, fc1_w) + fc1_b)
            h = jax.nn.relu(jnp.einsum('blh,gh->blg', h, fc2_w) + fc2_b)
            return jnp.einsum('blg,dg->bld', h, fc3_w) + fc3_b
        key = jax.random.key(seed)
        ks = jax.random.split(key, 16)
        g = lambda k, shape, s=0.02: jax.random.normal(k, shape, jnp.float32) * s
        A_init = jnp.broadcast_to(jnp.arange(1, D_STATE + 1, dtype=jnp.float32), (D_INNER, D_STATE))
        return {'x': jax.random.normal(ks[0], (B, L, D_MODEL), jnp.float32), 'rms1_w': jnp.ones((D_MODEL,), jnp.float32), 'rms2_w': jnp.ones((D_MODEL,), jnp.float32), 'in_proj_w': g(ks[1], (2 * D_INNER, D_MODEL)), 'conv_w': g(ks[2], (D_INNER, D_CONV), 0.1), 'conv_b': jnp.zeros((D_INNER,), jnp.float32), 'x_proj_w': g(ks[3], (DT_RANK + 2 * D_STATE, D_INNER)), 'dt_proj_w': g(ks[4], (D_INNER, DT_RANK), 0.1), 'dt_proj_b': jnp.full((D_INNER,), -4.0, jnp.float32), 'A_log': jnp.log(A_init), 'D_skip': jnp.ones((D_INNER,), jnp.float32), 'out_proj_w': g(ks[5], (D_MODEL, D_INNER)), 'fc1_w': g(ks[6], (2 * D_MODEL, D_MODEL)), 'fc1_b': jnp.zeros((2 * D_MODEL,), jnp.float32), 'fc2_w': g(ks[7], (2 * D_MODEL, 2 * D_MODEL)), 'fc2_b': jnp.zeros((2 * D_MODEL,), jnp.float32), 'fc3_w': g(ks[8], (D_MODEL, 2 * D_MODEL)), 'fc3_b': jnp.zeros((D_MODEL,), jnp.float32)}
    _L0_attn_a_in = _L0_attn_a_setup()

    def _L0_attn_b_setup():
        import jax, jax.numpy as jnp
        import numpy as np
        B, N, F_, H = (4, 256, 128, 16)
        DH = F_ // H
        SCALE = F_ / 19.5
        key = jax.random.key(seed)
        ks = jax.random.split(key, 9)
        s = 1.0 / np.sqrt(F_)
        return {'x': jax.random.normal(ks[0], (B, N, F_), jnp.float32), 'Wq': jax.random.normal(ks[1], (F_, F_), jnp.float32) * s, 'bq': jax.random.normal(ks[2], (F_,), jnp.float32) * s, 'Wk': jax.random.normal(ks[3], (F_, F_), jnp.float32) * s, 'bk': jax.random.normal(ks[4], (F_,), jnp.float32) * s, 'Wv': jax.random.normal(ks[5], (F_, F_), jnp.float32) * s, 'bv': jax.random.normal(ks[6], (F_,), jnp.float32) * s, 'Wo': jax.random.normal(ks[7], (F_, F_), jnp.float32) * s, 'bo': jax.random.normal(ks[8], (F_,), jnp.float32) * s}
    _L0_attn_b_in = _L0_attn_b_setup()

    def _L0_ffn_setup():
        import jax, jax.numpy as jnp
        import numpy as np
        THRESH_FACTOR = 0.7

        def ternary_quantize(w):
            delta = THRESH_FACTOR * jnp.mean(jnp.abs(w))
            return jnp.where(w > delta, 1.0, jnp.where(w < -delta, -1.0, 0.0)).astype(w.dtype)
        key = jax.random.key(seed)
        k1, k2, k3 = jax.random.split(key, 3)
        B, S, D_IN, D_OUT = (8, 512, 128, 128)
        inp = {'input': jax.random.normal(k1, (B, S, D_IN), dtype=jnp.float32), 'weight': jax.random.normal(k2, (D_OUT, D_IN), dtype=jnp.float32) * (1.0 / np.sqrt(D_IN)), 'alpha': jnp.ones((1,), dtype=jnp.float32), 'bias': jax.random.normal(k3, (D_OUT,), dtype=jnp.float32) * (1.0 / np.sqrt(D_IN))}
        return inp
    _L0_ffn_in = _L0_ffn_setup()

    def _L1_attn_a_setup():
        import jax, jax.numpy as jnp
        import numpy as np
        B, T, D_MODEL = (4, 512, 128)
        H = 16
        DH = D_MODEL // H
        EPS = 1e-06
        CHUNK = 128

        def _feature(x):
            return jnp.where(x > 0, x + 1.0, jnp.exp(x))

        def _causal_dot_product(Q, K, V):
            b, h, t, d = Q.shape
            nc = t // CHUNK
            mask = jnp.tril(jnp.ones((CHUNK, CHUNK), dtype=Q.dtype))
            qs = jnp.moveaxis(Q.reshape(b, h, nc, CHUNK, d), 2, 0)
            ks = jnp.moveaxis(K.reshape(b, h, nc, CHUNK, d), 2, 0)
            vs = jnp.moveaxis(V.reshape(b, h, nc, CHUNK, d), 2, 0)

            def step(S, qkv):
                q, k, v = qkv
                attn = jnp.einsum('bhid,bhjd->bhij', q, k) * mask
                out = jnp.einsum('bhij,bhjd->bhid', attn, v) + jnp.einsum('bhid,bhde->bhie', q, S)
                S = S + jnp.einsum('bhcd,bhce->bhde', k, v)
                return (S, out)
            S0 = jnp.zeros((b, h, d, d), dtype=Q.dtype)
            _, outs = jax.lax.scan(step, S0, (qs, ks, vs))
            return jnp.moveaxis(outs, 0, 2).reshape(b, h, t, d)
        key = jax.random.key(seed)
        ks = jax.random.split(key, 6)
        s = 0.02
        x = jax.random.normal(ks[0], (B, T, D_MODEL), dtype=jnp.float32)
        Wq = jax.random.normal(ks[1], (D_MODEL, D_MODEL), dtype=jnp.float32) * s
        Wk = jax.random.normal(ks[2], (D_MODEL, D_MODEL), dtype=jnp.float32) * s
        Wv = jax.random.normal(ks[3], (D_MODEL, D_MODEL), dtype=jnp.float32) * s
        Wo = jax.random.normal(ks[4], (D_MODEL, D_MODEL), dtype=jnp.float32) * s
        bo = jax.random.normal(ks[5], (D_MODEL,), dtype=jnp.float32) * s
        return {'x': x, 'Wq': Wq, 'Wk': Wk, 'Wv': Wv, 'Wo': Wo, 'bo': bo}
    _L1_attn_a_in = _L1_attn_a_setup()

    def _L1_attn_b_setup():
        import jax, jax.numpy as jnp
        import numpy as np
        HEAD_SIZE = 64
        key = jax.random.key(seed)
        ks = jax.random.split(key, 5)
        B, N, D, H, E, O = (2, 256, 128, 16, HEAD_SIZE, 128)
        return {'query': jax.random.normal(ks[0], (B, N, D), dtype=jnp.float32), 'Wq': jax.random.normal(ks[1], (H, D, E), dtype=jnp.float32) / np.sqrt(D), 'Wk': jax.random.normal(ks[2], (H, D, E), dtype=jnp.float32) / np.sqrt(D), 'Wv': jax.random.normal(ks[3], (H, D, E), dtype=jnp.float32) / np.sqrt(D), 'Wp': jax.random.normal(ks[4], (H * E, O), dtype=jnp.float32) / np.sqrt(H * E), 'bp': jnp.zeros((O,), dtype=jnp.float32)}
    _L1_attn_b_in = _L1_attn_b_setup()

    def _L1_ffn_setup():
        import jax, jax.numpy as jnp
        import numpy as np
        import math
        D_IN = 128
        FEATURES = (512, 512, 128)
        BATCH, SEQ = (8, 256)

        def _conn_dense(kernel_bool, x):
            w = jnp.where(kernel_bool, jnp.float32(1.0), jnp.float32(-1.0))
            return x @ w
        key = jax.random.key(seed)
        kx, kk0, kk1, kk2 = jax.random.split(key, 4)
        x = jax.random.normal(kx, (BATCH, SEQ, D_IN), dtype=jnp.float32)
        k0 = jax.random.randint(kk0, (2 * D_IN, FEATURES[0]), 0, 2).astype(jnp.bool_)
        k1 = jax.random.randint(kk1, (FEATURES[0], FEATURES[1]), 0, 2).astype(jnp.bool_)
        k2 = jax.random.randint(kk2, (FEATURES[1], FEATURES[2]), 0, 2).astype(jnp.bool_)
        s0 = jnp.asarray(1.0 / math.sqrt(2 * D_IN), dtype=jnp.float32)
        s1 = jnp.asarray(1.0 / math.sqrt(FEATURES[0]), dtype=jnp.float32)
        s2 = jnp.asarray(1.0 / math.sqrt(FEATURES[1]), dtype=jnp.float32)
        return {'x': x, 'k0': k0, 'k1': k1, 'k2': k2, 's0': s0, 's1': s1, 's2': s2}
    _L1_ffn_in = _L1_ffn_setup()

    def _L2_attn_a_setup():
        import jax, jax.numpy as jnp
        import numpy as np
        KEY_DIM = 128
        SCALE = KEY_DIM ** (-0.5)
        key = jax.random.key(seed)
        k1, k2, k3, k4 = jax.random.split(key, 4)
        B, S, E = (4, 256, 128)
        x = jax.random.normal(k1, (B, S, E), dtype=jnp.float32)
        WQ = jax.random.normal(k2, (KEY_DIM, E), dtype=jnp.float32) * E ** (-0.5)
        WK = jax.random.normal(k3, (KEY_DIM, E), dtype=jnp.float32) * E ** (-0.5)
        WV = jax.random.normal(k4, (KEY_DIM, E), dtype=jnp.float32) * E ** (-0.5)
        return {'x': x, 'WQ': WQ, 'WK': WK, 'WV': WV}
    _L2_attn_a_in = _L2_attn_a_setup()

    def _L2_attn_b_setup():
        import jax, jax.numpy as jnp
        import numpy as np
        N_HEADS = 16
        key = jax.random.key(seed)
        ks = jax.random.split(key, 9)
        B, S, D = (2, 256, 128)
        sc = 0.02
        return {'x': jax.random.normal(ks[0], (B, S, D), jnp.float32), 'Wq': jax.random.normal(ks[1], (D, D), jnp.float32) * sc, 'bq': jax.random.normal(ks[2], (D,), jnp.float32) * sc, 'Wk': jax.random.normal(ks[3], (D, D), jnp.float32) * sc, 'bk': jax.random.normal(ks[4], (D,), jnp.float32) * sc, 'Wv': jax.random.normal(ks[5], (D, D), jnp.float32) * sc, 'bv': jax.random.normal(ks[6], (D,), jnp.float32) * sc, 'Wo': jax.random.normal(ks[7], (D, D), jnp.float32) * sc, 'bo': jax.random.normal(ks[8], (D,), jnp.float32) * sc}
    _L2_attn_b_in = _L2_attn_b_setup()

    def _L2_ffn_setup():
        import jax, jax.numpy as jnp
        import numpy as np
        HIDDEN = 128
        FFN = 4 * HIDDEN
        NUM_EXPERTS = 8
        TOP_K = 2
        B, S = (4, 256)
        key = jax.random.key(seed)
        ks = jax.random.split(key, 7)
        scale = 0.02
        return {'x': jax.random.normal(ks[0], (B, S, HIDDEN), dtype=jnp.float32), 'gate_w': jax.random.normal(ks[1], (HIDDEN, NUM_EXPERTS), dtype=jnp.float32) * scale, 'gate_b': jnp.zeros((NUM_EXPERTS,), dtype=jnp.float32), 'w1': jax.random.normal(ks[2], (NUM_EXPERTS, HIDDEN, FFN), dtype=jnp.float32) * scale, 'b1': jnp.zeros((NUM_EXPERTS, FFN), dtype=jnp.float32), 'w2': jax.random.normal(ks[3], (NUM_EXPERTS, FFN, HIDDEN), dtype=jnp.float32) * scale, 'b2': jnp.zeros((NUM_EXPERTS, HIDDEN), dtype=jnp.float32)}
    _L2_ffn_in = _L2_ffn_setup()

    def _L3_attn_a_setup():
        import jax, jax.numpy as jnp
        import numpy as np
        D_MODEL = 128
        D_STATE = 16
        D_CONV = 4
        EXPAND = 2
        D_INNER = D_MODEL * EXPAND
        B, L = (4, 256)

        def _forward(x, norm_w, norm_b, W_in, conv_w, conv_b, x_proj_w, dt_w, dt_b, A_log, D, W_out):
            Bsz, Lln, _ = x.shape
            residual = x
            mu = jnp.mean(x, -1, keepdims=True)
            var = jnp.var(x, -1, keepdims=True)
            xn = (x - mu) * jax.lax.rsqrt(var + 1e-05) * norm_w + norm_b
            xz = xn @ W_in
            xc, z = jnp.split(xz, 2, axis=-1)
            x_pad = jnp.pad(xc, ((0, 0), (D_CONV - 1, 0), (0, 0)))
            xc = sum((x_pad[:, k:k + Lln, :] * conv_w[:, k] for k in range(D_CONV))) + conv_b
            xc = jax.nn.silu(xc)
            A = -jnp.exp(A_log)
            dbc = xc @ x_proj_w
            dt = jax.nn.softplus(dbc[..., :1] * dt_w + dt_b)
            Bp = dbc[..., 1:1 + D_STATE]
            Cp = dbc[..., 1 + D_STATE:]

            def step(h, inp):
                x_t, dt_t, B_t, C_t = inp
                A_bar = jnp.exp(dt_t[..., None] * A)
                h = A_bar * h + dt_t[..., None] * B_t[:, None, :] * x_t[..., None]
                y_t = jnp.einsum('bdn,bn->bd', h, C_t)
                return (h, y_t)
            h0 = jnp.zeros((Bsz, D_INNER, D_STATE), xc.dtype)
            xs = (jnp.moveaxis(xc, 1, 0), jnp.moveaxis(dt, 1, 0), jnp.moveaxis(Bp, 1, 0), jnp.moveaxis(Cp, 1, 0))
            _, ys = jax.lax.scan(step, h0, xs)
            y = jnp.moveaxis(ys, 0, 1) + xc * D
            y = y * jax.nn.silu(z)
            return y @ W_out + residual
        key = jax.random.key(seed)
        ks = jax.random.split(key, 12)
        s = lambda k, shape, fan: jax.random.normal(k, shape, jnp.float32) / np.sqrt(fan)
        return {'x': jax.random.normal(ks[0], (B, L, D_MODEL), jnp.float32), 'norm_w': jnp.ones((D_MODEL,), jnp.float32), 'norm_b': jnp.zeros((D_MODEL,), jnp.float32), 'W_in': s(ks[1], (D_MODEL, 2 * D_INNER), D_MODEL), 'conv_w': s(ks[2], (D_INNER, D_CONV), D_CONV), 'conv_b': jnp.zeros((D_INNER,), jnp.float32), 'x_proj_w': s(ks[3], (D_INNER, 2 * D_STATE + 1), D_INNER), 'dt_w': s(ks[4], (D_INNER,), 1), 'dt_b': jnp.zeros((D_INNER,), jnp.float32), 'A_log': jax.random.normal(ks[5], (D_INNER, D_STATE), jnp.float32) * 0.5, 'D': jnp.ones((D_INNER,), jnp.float32), 'W_out': s(ks[6], (D_INNER, D_MODEL), D_INNER)}
    _L3_attn_a_in = _L3_attn_a_setup()

    def _L3_attn_b_setup():
        import jax, jax.numpy as jnp
        import numpy as np
        H = 16

        def _eff_if_sorted(poids, Z):
            if poids.ndim == Z.ndim + 1:
                Zb = Z[..., None]
            else:
                Zb = Z
            a = jnp.cumsum(poids, axis=2)
            b = jnp.cumsum(poids * Zb, axis=2)
            return a * Zb - b
        key = jax.random.key(seed)
        ks = jax.random.split(key, 11)
        E = 128
        B, T = (4, 512)
        s = 1.0 / np.sqrt(E)
        return {'hidden_states': jax.random.normal(ks[0], (B, T, E), jnp.float32), 'Wq': jax.random.normal(ks[1], (E, E), jnp.float32) * s, 'bq': jax.random.normal(ks[2], (E,), jnp.float32) * 0.01, 'Wk': jax.random.normal(ks[3], (E, E), jnp.float32) * s, 'bk': jax.random.normal(ks[4], (E,), jnp.float32) * 0.01, 'Wv': jax.random.normal(ks[5], (E, E), jnp.float32) * s, 'bv': jax.random.normal(ks[6], (E,), jnp.float32) * 0.01, 'W1': jax.random.normal(ks[7], (E, E), jnp.float32) * s, 'b1': jax.random.normal(ks[8], (E,), jnp.float32) * 0.01, 'W2': jax.random.normal(ks[9], (E, H), jnp.float32) * s, 'b2': jax.random.normal(ks[10], (H,), jnp.float32) * 0.01}
    _L3_attn_b_in = _L3_attn_b_setup()

    def _L3_ffn_setup():
        import jax, jax.numpy as jnp
        import numpy as np
        DIM = 128
        HIDDEN = 384
        SCALE = 1.0 / 127.0

        def _dequant(w_int, dtype):
            return w_int.astype(dtype) * jnp.asarray(SCALE, dtype)
        key = jax.random.key(seed)
        k_x, k_g, k_u, k_d = jax.random.split(key, 4)
        x = jax.random.normal(k_x, (4, 256, DIM), dtype=jnp.float32)
        w_gate = jax.random.randint(k_g, (HIDDEN, DIM), -127, 128, dtype=jnp.int32)
        w_up = jax.random.randint(k_u, (HIDDEN, DIM), -127, 128, dtype=jnp.int32)
        w_down = jax.random.randint(k_d, (DIM, HIDDEN), -127, 128, dtype=jnp.int32)
        return {'x': x, 'w_gate': w_gate, 'w_up': w_up, 'w_down': w_down}
    _L3_ffn_in = _L3_ffn_setup()
    _d = {'L0_attn_a_x': _L0_attn_a_in['x'], 'L0_attn_a_rms1_w': _L0_attn_a_in['rms1_w'], 'L0_attn_a_rms2_w': _L0_attn_a_in['rms2_w'], 'L0_attn_a_in_proj_w': _L0_attn_a_in['in_proj_w'], 'L0_attn_a_conv_w': _L0_attn_a_in['conv_w'], 'L0_attn_a_conv_b': _L0_attn_a_in['conv_b'], 'L0_attn_a_x_proj_w': _L0_attn_a_in['x_proj_w'], 'L0_attn_a_dt_proj_w': _L0_attn_a_in['dt_proj_w'], 'L0_attn_a_dt_proj_b': _L0_attn_a_in['dt_proj_b'], 'L0_attn_a_A_log': _L0_attn_a_in['A_log'], 'L0_attn_a_D_skip': _L0_attn_a_in['D_skip'], 'L0_attn_a_out_proj_w': _L0_attn_a_in['out_proj_w'], 'L0_attn_a_fc1_w': _L0_attn_a_in['fc1_w'], 'L0_attn_a_fc1_b': _L0_attn_a_in['fc1_b'], 'L0_attn_a_fc2_w': _L0_attn_a_in['fc2_w'], 'L0_attn_a_fc2_b': _L0_attn_a_in['fc2_b'], 'L0_attn_a_fc3_w': _L0_attn_a_in['fc3_w'], 'L0_attn_a_fc3_b': _L0_attn_a_in['fc3_b'], 'L0_attn_b_Wq': _L0_attn_b_in['Wq'], 'L0_attn_b_bq': _L0_attn_b_in['bq'], 'L0_attn_b_Wk': _L0_attn_b_in['Wk'], 'L0_attn_b_bk': _L0_attn_b_in['bk'], 'L0_attn_b_Wv': _L0_attn_b_in['Wv'], 'L0_attn_b_bv': _L0_attn_b_in['bv'], 'L0_attn_b_Wo': _L0_attn_b_in['Wo'], 'L0_attn_b_bo': _L0_attn_b_in['bo'], 'L0_ffn_weight': _L0_ffn_in['weight'], 'L0_ffn_alpha': _L0_ffn_in['alpha'], 'L0_ffn_bias': _L0_ffn_in['bias'], 'L1_attn_a_Wq': _L1_attn_a_in['Wq'], 'L1_attn_a_Wk': _L1_attn_a_in['Wk'], 'L1_attn_a_Wv': _L1_attn_a_in['Wv'], 'L1_attn_a_Wo': _L1_attn_a_in['Wo'], 'L1_attn_a_bo': _L1_attn_a_in['bo'], 'L1_attn_b_Wq': _L1_attn_b_in['Wq'], 'L1_attn_b_Wk': _L1_attn_b_in['Wk'], 'L1_attn_b_Wv': _L1_attn_b_in['Wv'], 'L1_attn_b_Wp': _L1_attn_b_in['Wp'], 'L1_attn_b_bp': _L1_attn_b_in['bp'], 'L1_ffn_k0': _L1_ffn_in['k0'], 'L1_ffn_k1': _L1_ffn_in['k1'], 'L1_ffn_k2': _L1_ffn_in['k2'], 'L1_ffn_s0': _L1_ffn_in['s0'], 'L1_ffn_s1': _L1_ffn_in['s1'], 'L1_ffn_s2': _L1_ffn_in['s2'], 'L2_attn_a_WQ': _L2_attn_a_in['WQ'], 'L2_attn_a_WK': _L2_attn_a_in['WK'], 'L2_attn_a_WV': _L2_attn_a_in['WV'], 'L2_attn_b_Wq': _L2_attn_b_in['Wq'], 'L2_attn_b_bq': _L2_attn_b_in['bq'], 'L2_attn_b_Wk': _L2_attn_b_in['Wk'], 'L2_attn_b_bk': _L2_attn_b_in['bk'], 'L2_attn_b_Wv': _L2_attn_b_in['Wv'], 'L2_attn_b_bv': _L2_attn_b_in['bv'], 'L2_attn_b_Wo': _L2_attn_b_in['Wo'], 'L2_attn_b_bo': _L2_attn_b_in['bo'], 'L2_ffn_gate_w': _L2_ffn_in['gate_w'], 'L2_ffn_gate_b': _L2_ffn_in['gate_b'], 'L2_ffn_w1': _L2_ffn_in['w1'], 'L2_ffn_b1': _L2_ffn_in['b1'], 'L2_ffn_w2': _L2_ffn_in['w2'], 'L2_ffn_b2': _L2_ffn_in['b2'], 'L3_attn_a_norm_w': _L3_attn_a_in['norm_w'], 'L3_attn_a_norm_b': _L3_attn_a_in['norm_b'], 'L3_attn_a_W_in': _L3_attn_a_in['W_in'], 'L3_attn_a_conv_w': _L3_attn_a_in['conv_w'], 'L3_attn_a_conv_b': _L3_attn_a_in['conv_b'], 'L3_attn_a_x_proj_w': _L3_attn_a_in['x_proj_w'], 'L3_attn_a_dt_w': _L3_attn_a_in['dt_w'], 'L3_attn_a_dt_b': _L3_attn_a_in['dt_b'], 'L3_attn_a_A_log': _L3_attn_a_in['A_log'], 'L3_attn_a_D': _L3_attn_a_in['D'], 'L3_attn_a_W_out': _L3_attn_a_in['W_out'], 'L3_attn_b_Wq': _L3_attn_b_in['Wq'], 'L3_attn_b_bq': _L3_attn_b_in['bq'], 'L3_attn_b_Wk': _L3_attn_b_in['Wk'], 'L3_attn_b_bk': _L3_attn_b_in['bk'], 'L3_attn_b_Wv': _L3_attn_b_in['Wv'], 'L3_attn_b_bv': _L3_attn_b_in['bv'], 'L3_attn_b_W1': _L3_attn_b_in['W1'], 'L3_attn_b_b1': _L3_attn_b_in['b1'], 'L3_attn_b_W2': _L3_attn_b_in['W2'], 'L3_attn_b_b2': _L3_attn_b_in['b2'], 'L3_ffn_w_gate': _L3_ffn_in['w_gate'], 'L3_ffn_w_up': _L3_ffn_in['w_up'], 'L3_ffn_w_down': _L3_ffn_in['w_down']}
    _x0 = _d['L0_attn_a_x']
    _d['L0_attn_a_x'] = jax.random.normal(jax.random.fold_in(jax.random.key(seed), 1), (4, 512, 128), dtype=_x0.dtype)
    del _x0
    return _d

def reference(L0_attn_a_x, L0_attn_a_rms1_w, L0_attn_a_rms2_w, L0_attn_a_in_proj_w, L0_attn_a_conv_w, L0_attn_a_conv_b, L0_attn_a_x_proj_w, L0_attn_a_dt_proj_w, L0_attn_a_dt_proj_b, L0_attn_a_A_log, L0_attn_a_D_skip, L0_attn_a_out_proj_w, L0_attn_a_fc1_w, L0_attn_a_fc1_b, L0_attn_a_fc2_w, L0_attn_a_fc2_b, L0_attn_a_fc3_w, L0_attn_a_fc3_b, L0_attn_b_Wq, L0_attn_b_bq, L0_attn_b_Wk, L0_attn_b_bk, L0_attn_b_Wv, L0_attn_b_bv, L0_attn_b_Wo, L0_attn_b_bo, L0_ffn_weight, L0_ffn_alpha, L0_ffn_bias, L1_attn_a_Wq, L1_attn_a_Wk, L1_attn_a_Wv, L1_attn_a_Wo, L1_attn_a_bo, L1_attn_b_Wq, L1_attn_b_Wk, L1_attn_b_Wv, L1_attn_b_Wp, L1_attn_b_bp, L1_ffn_k0, L1_ffn_k1, L1_ffn_k2, L1_ffn_s0, L1_ffn_s1, L1_ffn_s2, L2_attn_a_WQ, L2_attn_a_WK, L2_attn_a_WV, L2_attn_b_Wq, L2_attn_b_bq, L2_attn_b_Wk, L2_attn_b_bk, L2_attn_b_Wv, L2_attn_b_bv, L2_attn_b_Wo, L2_attn_b_bo, L2_ffn_gate_w, L2_ffn_gate_b, L2_ffn_w1, L2_ffn_b1, L2_ffn_w2, L2_ffn_b2, L3_attn_a_norm_w, L3_attn_a_norm_b, L3_attn_a_W_in, L3_attn_a_conv_w, L3_attn_a_conv_b, L3_attn_a_x_proj_w, L3_attn_a_dt_w, L3_attn_a_dt_b, L3_attn_a_A_log, L3_attn_a_D, L3_attn_a_W_out, L3_attn_b_Wq, L3_attn_b_bq, L3_attn_b_Wk, L3_attn_b_bk, L3_attn_b_Wv, L3_attn_b_bv, L3_attn_b_W1, L3_attn_b_b1, L3_attn_b_W2, L3_attn_b_b2, L3_ffn_w_gate, L3_ffn_w_up, L3_ffn_w_down):

    def _L0_attn_a_ref(x, rms1_w, rms2_w, in_proj_w, conv_w, conv_b, x_proj_w, dt_proj_w, dt_proj_b, A_log, D_skip, out_proj_w, fc1_w, fc1_b, fc2_w, fc2_b, fc3_w, fc3_b):
        import jax, jax.numpy as jnp
        import numpy as np
        from jax import lax
        D_MODEL = 128
        D_INNER = 2 * D_MODEL
        D_STATE = 16
        D_CONV = 4
        DT_RANK = (D_MODEL + 15) // 16
        B, L = (4, 256)
        EPS = 1e-06

        def _rmsnorm(h, w):
            var = jnp.mean(h.astype(jnp.float32) ** 2, axis=-1, keepdims=True)
            return (w * (h * lax.rsqrt(var + EPS))).astype(h.dtype)

        def _mamba(x, in_proj_w, conv_w, conv_b, x_proj_w, dt_proj_w, dt_proj_b, A_log, D_skip, out_proj_w):
            xz = jnp.einsum('bld,ed->ble', x, in_proj_w)
            u, z = jnp.split(xz, 2, axis=-1)
            u_t = jnp.transpose(u, (0, 2, 1))
            conv = lax.conv_general_dilated(u_t, conv_w[:, None, :], (1,), [(D_CONV - 1, 0)], dimension_numbers=('NCH', 'OIH', 'NCH'), feature_group_count=D_INNER)
            u = jax.nn.silu(jnp.transpose(conv + conv_b[None, :, None], (0, 2, 1)))
            dbc = jnp.einsum('bld,ed->ble', u, x_proj_w)
            dt, Bm, Cm = jnp.split(dbc, [DT_RANK, DT_RANK + D_STATE], axis=-1)
            dt = jax.nn.softplus(jnp.einsum('blr,dr->bld', dt, dt_proj_w) + dt_proj_b)
            A = -jnp.exp(A_log)

            def step(s, inp):
                d, u_i, b_i, c_i = inp
                s = s * jnp.exp(d[..., None] * A) + (d * u_i)[..., None] * b_i[:, None, :]
                y = jnp.einsum('bdn,bn->bd', s, c_i)
                return (s, y)
            s0 = jnp.zeros((u.shape[0], D_INNER, D_STATE), u.dtype)
            inputs = (jnp.moveaxis(dt, 1, 0), jnp.moveaxis(u, 1, 0), jnp.moveaxis(Bm, 1, 0), jnp.moveaxis(Cm, 1, 0))
            _, ys = lax.scan(step, s0, inputs)
            y = jnp.moveaxis(ys, 0, 1) + u * D_skip
            y = y * jax.nn.silu(z)
            return jnp.einsum('ble,de->bld', y, out_proj_w)

        def _mlp(x, fc1_w, fc1_b, fc2_w, fc2_b, fc3_w, fc3_b):
            h = jax.nn.relu(jnp.einsum('bld,hd->blh', x, fc1_w) + fc1_b)
            h = jax.nn.relu(jnp.einsum('blh,gh->blg', h, fc2_w) + fc2_b)
            return jnp.einsum('blg,dg->bld', h, fc3_w) + fc3_b
        x0 = _rmsnorm(x, rms1_w)
        x1 = _mamba(x0, in_proj_w, conv_w, conv_b, x_proj_w, dt_proj_w, dt_proj_b, A_log, D_skip, out_proj_w)
        x = x1 + x
        x2 = _rmsnorm(x, rms2_w)
        x3 = _mlp(x2, fc1_w, fc1_b, fc2_w, fc2_b, fc3_w, fc3_b)
        return x + x3

    def _L0_attn_b_ref(x, Wq, bq, Wk, bk, Wv, bv, Wo, bo):
        import jax, jax.numpy as jnp
        import numpy as np
        B, N, F_, H = (4, 256, 128, 16)
        DH = F_ // H
        SCALE = F_ / 19.5
        b, n, f = x.shape

        def proj(W, bias):
            return (x @ W.T + bias).reshape(b, n, H, DH).transpose(0, 2, 1, 3)
        q = proj(Wq, bq)
        k = proj(Wk, bk)
        v = proj(Wv, bv)
        score = jax.nn.softmax(jnp.einsum('bhif,bhjf->bhij', q, k) / SCALE, axis=-1)
        attn = jnp.einsum('bhij,bhjf->bihf', score, v)
        o = attn.reshape(b, n, f) @ Wo.T + bo
        return o

    def _L0_ffn_ref(input, weight, alpha, bias):
        import jax, jax.numpy as jnp
        import numpy as np
        THRESH_FACTOR = 0.7

        def ternary_quantize(w):
            delta = THRESH_FACTOR * jnp.mean(jnp.abs(w))
            return jnp.where(w > delta, 1.0, jnp.where(w < -delta, -1.0, 0.0)).astype(w.dtype)
        w_ternary = ternary_quantize(weight)
        w_eff = w_ternary * alpha
        out = jnp.einsum('bsd,od->bso', input, w_eff) + bias
        return out

    def _L1_attn_a_ref(x, Wq, Wk, Wv, Wo, bo):
        import jax, jax.numpy as jnp
        import numpy as np
        B, T, D_MODEL = (4, 512, 128)
        H = 16
        DH = D_MODEL // H
        EPS = 1e-06
        CHUNK = 128

        def _feature(x):
            return jnp.where(x > 0, x + 1.0, jnp.exp(x))

        def _causal_dot_product(Q, K, V):
            b, h, t, d = Q.shape
            nc = t // CHUNK
            mask = jnp.tril(jnp.ones((CHUNK, CHUNK), dtype=Q.dtype))
            qs = jnp.moveaxis(Q.reshape(b, h, nc, CHUNK, d), 2, 0)
            ks = jnp.moveaxis(K.reshape(b, h, nc, CHUNK, d), 2, 0)
            vs = jnp.moveaxis(V.reshape(b, h, nc, CHUNK, d), 2, 0)

            def step(S, qkv):
                q, k, v = qkv
                attn = jnp.einsum('bhid,bhjd->bhij', q, k) * mask
                out = jnp.einsum('bhij,bhjd->bhid', attn, v) + jnp.einsum('bhid,bhde->bhie', q, S)
                S = S + jnp.einsum('bhcd,bhce->bhde', k, v)
                return (S, out)
            S0 = jnp.zeros((b, h, d, d), dtype=Q.dtype)
            _, outs = jax.lax.scan(step, S0, (qs, ks, vs))
            return jnp.moveaxis(outs, 0, 2).reshape(b, h, t, d)
        b, t, _ = x.shape

        def proj(W):
            return (x @ W).reshape(b, t, H, DH).transpose(0, 2, 1, 3)
        Q = _feature(proj(Wq))
        K = _feature(proj(Wk))
        V = proj(Wv)
        Z = 1.0 / (jnp.einsum('bhtd,bhtd->bht', Q, jnp.cumsum(K, axis=1)) + EPS)
        unnorm = _causal_dot_product(Q, K, V)
        out = unnorm * Z[..., None]
        out = out.transpose(0, 2, 1, 3).reshape(b, t, H * DH)
        return out @ Wo + bo

    def _L1_attn_b_ref(query, Wq, Wk, Wv, Wp, bp):
        import jax, jax.numpy as jnp
        import numpy as np
        HEAD_SIZE = 64
        B, N, D = query.shape
        H, _, E = Wq.shape
        scale = 1.0 / jnp.sqrt(jnp.asarray(E, query.dtype))
        q = jnp.einsum('bnd,hde->bhne', query, Wq) * scale
        k = jnp.einsum('bmd,hde->bhme', query, Wk)
        v = jnp.einsum('bmd,hde->bhme', query, Wv)
        logits = jnp.einsum('bhne,bhme->bhnm', q, k)
        attn = jax.nn.softmax(logits, axis=-1)
        out = jnp.einsum('bhnm,bhme->bnhe', attn, v)
        out = jnp.swapaxes(out, -1, -2).reshape(B, N, E * H)
        return jnp.dot(out, Wp) + bp

    def _L1_ffn_ref(x, k0, k1, k2, s0, s1, s2):
        import jax, jax.numpy as jnp
        import numpy as np
        import math
        D_IN = 128
        FEATURES = (512, 512, 128)
        BATCH, SEQ = (8, 256)

        def _conn_dense(kernel_bool, x):
            w = jnp.where(kernel_bool, jnp.float32(1.0), jnp.float32(-1.0))
            return x @ w
        h = jnp.concatenate([x, -x], axis=-1)
        h = s0 * _conn_dense(k0, h)
        h = jax.nn.relu(h) * 2
        h = s1 * _conn_dense(k1, h)
        h = jax.nn.relu(h) * 2
        h = s2 * _conn_dense(k2, h)
        return h

    def _L2_attn_a_ref(x, WQ, WK, WV):
        import jax, jax.numpy as jnp
        import numpy as np
        KEY_DIM = 128
        SCALE = KEY_DIM ** (-0.5)
        q = jnp.einsum('bse,ke->bsk', x, WQ)
        k = jnp.einsum('bse,ke->bsk', x, WK)
        v = jnp.einsum('bse,ve->bsv', x, WV)
        scores = jnp.einsum('bsk,btk->bst', q, k) * SCALE
        masked = jnp.where(jnp.tril(scores) == 0, -jnp.inf, scores)
        attn = jax.nn.softmax(masked, axis=-1)
        return jnp.einsum('bst,btv->bsv', attn, v)

    def _L2_attn_b_ref(x, Wq, bq, Wk, bk, Wv, bv, Wo, bo):
        import jax, jax.numpy as jnp
        import numpy as np
        N_HEADS = 16
        B, S, D = x.shape
        H = N_HEADS
        hd = D // H

        def proj(W, b):
            y = jnp.einsum('bsd,ed->bse', x, W) + b
            return y.reshape(B, S, H, hd).transpose(0, 2, 1, 3)
        q = proj(Wq, bq)
        k = proj(Wk, bk)
        v = proj(Wv, bv)
        scores = jnp.einsum('bhqd,bhkd->bhqk', q, k) / jnp.sqrt(jnp.asarray(hd, x.dtype))
        causal = jnp.tril(jnp.ones((S, S), dtype=bool))
        scores = jnp.where(causal[None, None], scores, jnp.asarray(-jnp.inf, scores.dtype))
        attn = jax.nn.softmax(scores, axis=-1)
        ctx = jnp.einsum('bhqk,bhkd->bhqd', attn, v)
        ctx = ctx.transpose(0, 2, 1, 3).reshape(B, S, D)
        out = jnp.einsum('bsd,ed->bse', ctx, Wo) + bo
        return out

    def _L2_ffn_ref(x, gate_w, gate_b, w1, b1, w2, b2):
        import jax, jax.numpy as jnp
        import numpy as np
        HIDDEN = 128
        FFN = 4 * HIDDEN
        NUM_EXPERTS = 8
        TOP_K = 2
        B, S = (4, 256)
        b, s, h = x.shape
        xt = x.reshape(b * s, h)
        probs = jax.nn.softmax(xt @ gate_w + gate_b, axis=-1)
        _, idx = jax.lax.top_k(probs, TOP_K)
        one_hot = jax.nn.one_hot(idx, NUM_EXPERTS, dtype=xt.dtype)
        mask = (one_hot.sum(axis=1) > 0).astype(xt.dtype)
        h1 = jax.nn.relu(jnp.einsum('th,ehf->etf', xt, w1) + b1[:, None, :])
        out_e = jnp.einsum('etf,efh->eth', h1, w2) + b2[:, None, :]
        out = jnp.einsum('eth,te->th', out_e, mask)
        return out.reshape(b, s, h)

    def _L3_attn_a_ref(x, norm_w, norm_b, W_in, conv_w, conv_b, x_proj_w, dt_w, dt_b, A_log, D, W_out):
        import jax, jax.numpy as jnp
        import numpy as np
        D_MODEL = 128
        D_STATE = 16
        D_CONV = 4
        EXPAND = 2
        D_INNER = D_MODEL * EXPAND
        B, L = (4, 256)

        def _forward(x, norm_w, norm_b, W_in, conv_w, conv_b, x_proj_w, dt_w, dt_b, A_log, D, W_out):
            Bsz, Lln, _ = x.shape
            residual = x
            mu = jnp.mean(x, -1, keepdims=True)
            var = jnp.var(x, -1, keepdims=True)
            xn = (x - mu) * jax.lax.rsqrt(var + 1e-05) * norm_w + norm_b
            xz = xn @ W_in
            xc, z = jnp.split(xz, 2, axis=-1)
            x_pad = jnp.pad(xc, ((0, 0), (D_CONV - 1, 0), (0, 0)))
            xc = sum((x_pad[:, k:k + Lln, :] * conv_w[:, k] for k in range(D_CONV))) + conv_b
            xc = jax.nn.silu(xc)
            A = -jnp.exp(A_log)
            dbc = xc @ x_proj_w
            dt = jax.nn.softplus(dbc[..., :1] * dt_w + dt_b)
            Bp = dbc[..., 1:1 + D_STATE]
            Cp = dbc[..., 1 + D_STATE:]

            def step(h, inp):
                x_t, dt_t, B_t, C_t = inp
                A_bar = jnp.exp(dt_t[..., None] * A)
                h = A_bar * h + dt_t[..., None] * B_t[:, None, :] * x_t[..., None]
                y_t = jnp.einsum('bdn,bn->bd', h, C_t)
                return (h, y_t)
            h0 = jnp.zeros((Bsz, D_INNER, D_STATE), xc.dtype)
            xs = (jnp.moveaxis(xc, 1, 0), jnp.moveaxis(dt, 1, 0), jnp.moveaxis(Bp, 1, 0), jnp.moveaxis(Cp, 1, 0))
            _, ys = jax.lax.scan(step, h0, xs)
            y = jnp.moveaxis(ys, 0, 1) + xc * D
            y = y * jax.nn.silu(z)
            return y @ W_out + residual
        return _forward(x, norm_w, norm_b, W_in, conv_w, conv_b, x_proj_w, dt_w, dt_b, A_log, D, W_out)

    def _L3_attn_b_ref(hidden_states, Wq, bq, Wk, bk, Wv, bv, W1, b1, W2, b2):
        import jax, jax.numpy as jnp
        import numpy as np
        H = 16

        def _eff_if_sorted(poids, Z):
            if poids.ndim == Z.ndim + 1:
                Zb = Z[..., None]
            else:
                Zb = Z
            a = jnp.cumsum(poids, axis=2)
            b = jnp.cumsum(poids * Zb, axis=2)
            return a * Zb - b
        B, T, E = hidden_states.shape
        D = E // H

        def heads(x):
            return x.reshape(B, T, H, D).transpose(0, 2, 1, 3)
        q = heads(hidden_states @ Wq + bq)
        k = heads(hidden_states @ Wk + bk)
        v = heads(hidden_states @ Wv + bv)

        def proj(x4):
            x = x4.reshape(B, T, H * D)
            m = jax.nn.gelu(x @ W1 + b1, approximate=False)
            return m @ W2 + b2
        q_proj = proj(q)
        k_proj = proj(k)
        eps = 1e-06
        mean_q = jnp.mean(q_proj, axis=1, keepdims=True)
        mean_k = jnp.mean(k_proj, axis=1, keepdims=True)
        qc = q_proj - mean_q
        kc = k_proj - mean_k
        var_q = jnp.mean(qc ** 2, axis=1, keepdims=True)
        var_k = jnp.mean(kc ** 2, axis=1, keepdims=True)
        std = jnp.sqrt(0.5 * (var_q + var_k) + eps)
        q_proj = qc / std
        k_proj = kc / std
        Z = jnp.concatenate([k_proj, q_proj], axis=1).transpose(0, 2, 1)
        idx = jnp.argsort(Z, axis=2)
        Z_sort = jnp.take_along_axis(Z, idx, axis=2)
        inv = jnp.argsort(idx, axis=2)
        vc = v - jnp.mean(v, axis=2, keepdims=True)
        v_exp = jnp.concatenate([vc, jnp.zeros_like(vc)], axis=2)
        v_sorted = jnp.take_along_axis(v_exp, idx[..., None], axis=2)
        context_s = _eff_if_sorted(v_sorted, Z_sort)
        context = jnp.take_along_axis(context_s, inv[..., None], axis=2)[:, :, T:]
        v_norm = jnp.concatenate([jnp.ones((B, H, T), Z.dtype), jnp.zeros((B, H, T), Z.dtype)], axis=2)
        vns = jnp.take_along_axis(v_norm, idx, axis=2)
        sum_relu = _eff_if_sorted(vns, Z_sort)
        total_v = jnp.sum(vns, axis=2, keepdims=True)
        total_vz = jnp.sum(vns * Z_sort, axis=2, keepdims=True)
        norm_sorted = 2.0 * sum_relu - (Z_sort * total_v - total_vz)
        norm = jnp.take_along_axis(norm_sorted, inv, axis=2)[:, :, T:]
        norm = jnp.maximum(norm, 0.0001)
        context = 2.0 * context / norm[..., None]
        return context.transpose(0, 2, 1, 3).reshape(B, T, H * D)

    def _L3_ffn_ref(x, w_gate, w_up, w_down):
        import jax, jax.numpy as jnp
        import numpy as np
        DIM = 128
        HIDDEN = 384
        SCALE = 1.0 / 127.0

        def _dequant(w_int, dtype):
            return w_int.astype(dtype) * jnp.asarray(SCALE, dtype)
        wg = _dequant(w_gate, x.dtype)
        wu = _dequant(w_up, x.dtype)
        wd = _dequant(w_down, x.dtype)
        gate = jnp.einsum('bsd,hd->bsh', x, wg)
        up = jnp.einsum('bsd,hd->bsh', x, wu)
        h = jax.nn.silu(gate) * up
        return jnp.einsum('bsh,dh->bsd', h, wd)
    x = L0_attn_a_x
    x = x + _L0_attn_a_ref(_layernorm(x, axis=-1), L0_attn_a_rms1_w, L0_attn_a_rms2_w, L0_attn_a_in_proj_w, L0_attn_a_conv_w, L0_attn_a_conv_b, L0_attn_a_x_proj_w, L0_attn_a_dt_proj_w, L0_attn_a_dt_proj_b, L0_attn_a_A_log, L0_attn_a_D_skip, L0_attn_a_out_proj_w, L0_attn_a_fc1_w, L0_attn_a_fc1_b, L0_attn_a_fc2_w, L0_attn_a_fc2_b, L0_attn_a_fc3_w, L0_attn_a_fc3_b)
    x = x + _L0_ffn_ref(_layernorm(x, axis=-1), L0_ffn_weight, L0_ffn_alpha, L0_ffn_bias)
    x = x + _L0_attn_b_ref(_layernorm(x, axis=-1), L0_attn_b_Wq, L0_attn_b_bq, L0_attn_b_Wk, L0_attn_b_bk, L0_attn_b_Wv, L0_attn_b_bv, L0_attn_b_Wo, L0_attn_b_bo)
    x = x + _L0_ffn_ref(_layernorm(x, axis=-1), L0_ffn_weight, L0_ffn_alpha, L0_ffn_bias)
    x = x + _L1_attn_a_ref(_layernorm(x, axis=-1), L1_attn_a_Wq, L1_attn_a_Wk, L1_attn_a_Wv, L1_attn_a_Wo, L1_attn_a_bo)
    x = x + _L1_ffn_ref(_layernorm(x, axis=-1), L1_ffn_k0, L1_ffn_k1, L1_ffn_k2, L1_ffn_s0, L1_ffn_s1, L1_ffn_s2)
    x = x + _L1_attn_b_ref(_layernorm(x, axis=-1), L1_attn_b_Wq, L1_attn_b_Wk, L1_attn_b_Wv, L1_attn_b_Wp, L1_attn_b_bp)
    x = x + _L1_ffn_ref(_layernorm(x, axis=-1), L1_ffn_k0, L1_ffn_k1, L1_ffn_k2, L1_ffn_s0, L1_ffn_s1, L1_ffn_s2)
    x = x + _L2_attn_a_ref(_layernorm(x, axis=-1), L2_attn_a_WQ, L2_attn_a_WK, L2_attn_a_WV)
    x = x + _L2_ffn_ref(_layernorm(x, axis=-1), L2_ffn_gate_w, L2_ffn_gate_b, L2_ffn_w1, L2_ffn_b1, L2_ffn_w2, L2_ffn_b2)
    x = x + _L2_attn_b_ref(_layernorm(x, axis=-1), L2_attn_b_Wq, L2_attn_b_bq, L2_attn_b_Wk, L2_attn_b_bk, L2_attn_b_Wv, L2_attn_b_bv, L2_attn_b_Wo, L2_attn_b_bo)
    x = x + _L2_ffn_ref(_layernorm(x, axis=-1), L2_ffn_gate_w, L2_ffn_gate_b, L2_ffn_w1, L2_ffn_b1, L2_ffn_w2, L2_ffn_b2)
    x = x + _L3_attn_a_ref(_layernorm(x, axis=-1), L3_attn_a_norm_w, L3_attn_a_norm_b, L3_attn_a_W_in, L3_attn_a_conv_w, L3_attn_a_conv_b, L3_attn_a_x_proj_w, L3_attn_a_dt_w, L3_attn_a_dt_b, L3_attn_a_A_log, L3_attn_a_D, L3_attn_a_W_out)
    x = x + _L3_ffn_ref(_layernorm(x, axis=-1), L3_ffn_w_gate, L3_ffn_w_up, L3_ffn_w_down)
    x = x + _L3_attn_b_ref(_layernorm(x, axis=-1), L3_attn_b_Wq, L3_attn_b_bq, L3_attn_b_Wk, L3_attn_b_bk, L3_attn_b_Wv, L3_attn_b_bv, L3_attn_b_W1, L3_attn_b_b1, L3_attn_b_W2, L3_attn_b_b2)
    x = x + _L3_ffn_ref(_layernorm(x, axis=-1), L3_ffn_w_gate, L3_ffn_w_up, L3_ffn_w_down)
    return x

_drawn_inputs = setup_inputs


def setup_inputs(seed=0):
    import zlib

    import numpy as np

    out = dict(_drawn_inputs(seed))
    spreads = {'L0_attn_a_rms1_w': (1.0, 0.2),
     'L0_attn_a_rms2_w': (1.0, 0.2),
     'L0_attn_a_conv_b': (0.0, 0.1),
     'L0_attn_a_dt_proj_b': (-4.0, 0.2),
     'L0_attn_a_D_skip': (1.0, 0.2),
     'L0_attn_a_fc1_b': (0.0, 0.1),
     'L0_attn_a_fc2_b': (0.0, 0.1),
     'L0_attn_a_fc3_b': (0.0, 0.1),
     'L1_attn_b_bp': (0.0, 0.1),
     'L2_ffn_gate_b': (0.0, 0.1),
     'L2_ffn_b1': (0.0, 0.1),
     'L2_ffn_b2': (0.0, 0.1),
     'L3_attn_a_norm_w': (1.0, 0.2),
     'L3_attn_a_norm_b': (0.0, 0.1),
     'L3_attn_a_conv_b': (0.0, 0.1),
     'L3_attn_a_dt_b': (0.0, 0.1),
     'L3_attn_a_D': (1.0, 0.2)}
    factors = {}
    for name, (base, spread) in spreads.items():
        noise = np.random.default_rng([zlib.crc32(name.encode()), seed]).standard_normal(out[name].shape)
        drawn = base * np.exp(spread * noise) if base else spread * noise
        out[name] = jnp.asarray(drawn.astype(out[name].dtype))
    for name, factor in factors.items():
        out[name] = (out[name] * factor).astype(out[name].dtype)
    return out
```

```python
from contextlib import ExitStack

import concourse.bass as bass
from concourse import mybir

P = 128
BATCH = 4
T = 512
NB = 2
H = 16
DH = P // H
KT = T // P
DI = 2 * P
NS = 16
E = 8
FF = 4 * P
FT = FF // P
HE = 64
HID = 3 * P
NEG = -1e30

ALU = mybir.AluOpType
ACT = mybir.ActivationFunctionType
F32 = mybir.dt.float32
BF16 = mybir.dt.bfloat16
I32 = mybir.dt.int32
U8 = mybir.dt.uint8
AX = mybir.AxisListType


class Net:

    def __init__(self, nc, ctx, cols):
        self.nc, self.ctx, self.cols = nc, ctx, cols
        self.spent, self.spent_ctx = [], ExitStack()

    def w(self, name, a=0, n=None):
        rows, c0, width = self.cols[name]
        return self.weights[0:rows, c0 + a:c0 + a + (width - a if n is None else n)]


class Stage:

    def __init__(self, g, name):
        self.g, self.nc, self.name, self.sems = g, g.nc, name, []

    def __enter__(self):
        self.ctx, self.sem_ctx = ExitStack(), ExitStack()
        self.to_clear = self.g.spent
        return self

    def __exit__(self, *error):
        self.ctx.close()
        self.g.spent_ctx.close()
        self.g.spent, self.g.spent_ctx = self.sems, self.sem_ctx

    def sem(self, name):
        s = self.sem_ctx.enter_context(self.nc.semaphore(f"{self.name}_{name}"))
        self.sems.append(s)
        return s

    def sb(self, name, shape, dt=F32):
        return self.ctx.enter_context(self.nc.sbuf_tensor(f"{self.name}_{name}", shape, dt))

    def clear_spent(self, sp):
        for s in self.to_clear:
            sp.sem_clear(s)


def bcast(ap, dim, n):
    a = [list(x) for x in ap.ap]
    a.insert(dim, [0, n])
    return bass.AP(tensor=ap.tensor, offset=ap.offset, ap=a)


def widen(col, n):
    return bass.AP(tensor=col.tensor, offset=col.offset, ap=[list(col.ap[0]), [0, n]])


class Norm:

    def __init__(self, st, mean_bank, var_bank, out=None):
        self.g, self.mb, self.vb = st.g, mean_bank, var_bank
        self.out = out if out is not None else st.g.xn
        self.xc = st.sb("ln_xc", [P, NB, T])
        self.sq = st.sb("ln_sq", [P, NB, T])
        self.mean = st.sem("ln_mean")
        self.centred = st.sem("ln_centred")
        self.squared = st.sem("ln_squared")
        self.var = st.sem("ln_var")
        self.log = st.sem("ln_log")
        self.rstd = st.sem("ln_rstd")
        self.done = st.sem("ln_done")

    def tensor(self, pe):
        g = self.g
        for b in range(NB):
            pe.matmul(g.ps[:, self.mb[b], :], g.w("mean_mat"), g.xs[:, b, :], start=True, stop=True).then_inc(self.mean, 1)
        for b in range(NB):
            pe.wait_ge(self.squared, b + 1)
            pe.matmul(g.ps[:, self.vb[b], :], g.w("mean_mat"), self.sq[:, b, :], start=True, stop=True).then_inc(self.var, 1)

    def scalar(self, act):
        g = self.g
        for b in range(NB):
            act.wait_ge(self.centred, b + 1)
            act.activation(self.sq[:, b, :], self.xc[:, b, :], ACT.Square).then_inc(self.squared, 1)
        for b in range(NB):
            act.wait_ge(self.var, b + 1)
            act.activation(self.sq[:, b, :], g.ps[:, self.vb[b], :], ACT.Ln, bias=g.w("eps5")).then_inc(self.log, 1)
            act.wait_ge(self.log, b + 1)
            act.activation(self.sq[:, b, :], self.sq[:, b, :], ACT.Exp, scale=-0.5).then_inc(self.rstd, 1)

    def vector(self, dve):
        g = self.g
        for b in range(NB):
            dve.wait_ge(self.mean, b + 1)
            dve.tensor_tensor(self.xc[:, b, :], g.xs[:, b, :], g.ps[:, self.mb[b], :], ALU.subtract).then_inc(self.centred, 1)
        for b in range(NB):
            dve.wait_ge(self.rstd, b + 1)
            dve.tensor_tensor(self.out[:, b, :], self.xc[:, b, :], self.sq[:, b, :], ALU.mult).then_inc(self.done, 1)


def prepare(g, wd, boold, intd):
    nc = g.nc
    with Stage(g, "prep") as st:
        n = g.weights.shape[1]
        cut = 8
        step = -(-n // cut)
        bools = st.sb("bools", [P, boold.shape[1]], U8)
        ints = st.sb("ints", [P, intd.shape[1]], I32)
        absum = st.sb("absum", [P, 1])
        thr = st.sb("thr", [P, 2])
        low = st.sb("low", [P, P])
        loaded, bools_in, ints_in = st.sem("loaded"), st.sem("bools_in"), st.sem("ints_in")
        summed, total, thr_ready, steps = st.sem("summed"), st.sem("total"), st.sem("thr_ready"), st.sem("steps")
        a_ready = st.sem("a_ready")
        with nc.Block() as block:
            @block.sync
            def _(sp):
                for c in range(cut):
                    a, z = c * step, min(n, (c + 1) * step)
                    sp.dma_start(g.weights[:, a:z], wd[:, a:z]).then_inc(loaded, 16)
                sp.dma_start(bools[:, :], boold).then_inc(bools_in, 16)
                sp.dma_start(ints[:, :], intd).then_inc(ints_in, 16)

            @block.vector
            def _(dve):
                dve.wait_ge(loaded, 16 * cut)
                dve.tensor_reduce(absum[:, :], g.w("f0_w"), AX.X, ALU.add, apply_absolute_value=True).then_inc(summed, 1)
                dve.wait_ge(total, 1)
                dve.tensor_scalar(thr[:, 0:1], g.ps[:, 0, 0:1], 1.0 / P, 0.7, ALU.mult, ALU.mult).then_inc(thr_ready, 1)
                dve.wait_ge(thr_ready, 1)
                dve.tensor_scalar(thr[:, 1:2], thr[:, 0:1], -1.0, None, ALU.mult).then_inc(thr_ready, 1)
                dve.wait_ge(thr_ready, 2)
                dve.tensor_scalar(low[:, :], g.w("f0_w"), thr[:, 1:2], None, ALU.is_lt).then_inc(steps, 1)
                dve.tensor_scalar(g.tern[:, :], g.w("f0_w"), thr[:, 0:1], None, ALU.is_gt).then_inc(steps, 1)
                dve.wait_ge(steps, 2)
                dve.tensor_tensor(g.tern[:, :], g.tern[:, :], low[:, :], ALU.subtract).then_inc(steps, 1)
                dve.wait_ge(steps, 3)
                dve.tensor_scalar(g.tern[:, :], g.tern[:, :], g.w("f0_alpha"), None, ALU.mult).then_inc(steps, 1)
                dve.wait_ge(bools_in, 16)
                dve.tensor_copy(g.conn[:, :], bools[:, FF:]).then_inc(steps, 1)
                dve.wait_ge(steps, 5)
                dve.tensor_tensor(g.conn[:, 0:FF], bools[:, 0:FF], g.conn[:, 0:FF], ALU.subtract).then_inc(steps, 1)
                dve.wait_ge(steps, 6)
                dve.tensor_scalar(g.conn[:, 0:FF], g.conn[:, 0:FF], 2.0, None, ALU.mult).then_inc(steps, 1)
                dve.tensor_scalar(g.conn[:, FF:], g.conn[:, FF:], 2.0, 1.0, ALU.mult, ALU.subtract).then_inc(steps, 1)
                dve.tensor_scalar(g.s2x[:, :], g.w("f1_s", 0, 2), 2.0, None, ALU.mult).then_inc(steps, 1)
                dve.wait_ge(ints_in, 16)
                dve.tensor_copy(g.gated[:, :], ints[:, :]).then_inc(steps, 1)
                dve.wait_ge(steps, 10)
                dve.tensor_scalar(g.gated[:, :], g.gated[:, :], 1.0 / 127.0, None, ALU.mult).then_inc(steps, 1)
                dve.tensor_copy(g.cb[:, :], g.w("bf_consts")).then_inc(steps, 1)

            @block.tensor
            def _(pe):
                pe.wait_ge(summed, 1)
                pe.matmul(g.ps[:, 0, 0:1], g.w("mean_mat"), absum[:, :], start=True, stop=True).then_inc(total, 1)

            @block.scalar
            def _(act):
                act.wait_ge(loaded, 16 * cut)
                for k, name in enumerate(("m0_alog", "m3_alog")):
                    act.activation(g.A[:, k, :], g.w(name), ACT.Exp).then_inc(a_ready, 1)
                act.wait_ge(a_ready, 2)
                act.activation(g.A[:, :, :], g.A[:, :, :], ACT.Copy, scale=-1.0).then_inc(a_ready, 1)


def load_x(g, x_dram, i):
    with Stage(g, "load") as st:
        landed = st.sem("landed")
        with g.nc.Block() as block:
            @block.sync
            def _(sp):
                st.clear_spent(sp)
                sp.sem_clear(g.stored)
                sp.dma_start(g.xs[:, :, :], x_dram[bass.ds(i * NB, NB), :, :].rearrange("b p t -> p b t")).then_inc(landed, 16)
                sp.wait_ge(landed, 16)


def store_x(g, out_dram, i):
    with Stage(g, "store") as st:
        with g.nc.Block() as block:
            @block.sync
            def _(sp):
                st.clear_spent(sp)
                sp.dma_start(out_dram[bass.ds(i * NB, NB), :, :].rearrange("b p t -> p b t"), g.xs[:, :, :]).then_inc(g.stored, 16)
                sp.wait_ge(g.stored, 16)


def ternary_ffn(g, name):
    with Stage(g, name) as st:
        ln = Norm(st, (0, 1), (2, 3))
        out_ready, added = st.sem("out_ready"), st.sem("added")
        with g.nc.Block() as block:
            @block.sync
            def _(sp):
                st.clear_spent(sp)

            @block.tensor
            def _(pe):
                ln.tensor(pe)
                for b in range(NB):
                    pe.wait_ge(ln.done, b + 1)
                    pe.matmul(g.ps[:, 4 + b, :], g.tern[:, :], g.xn[:, b, :], start=True, stop=True).then_inc(out_ready, 1)

            @block.scalar
            def _(act):
                ln.scalar(act)

            @block.vector
            def _(dve):
                ln.vector(dve)
                for b in range(NB):
                    dve.wait_ge(out_ready, b + 1)
                    dve.scalar_tensor_tensor(out=g.xs[:, b, :], in0=g.ps[:, 4 + b, :], scalar=g.w("f0_b"), in1=g.xs[:, b, :],
                                             op0=ALU.add, op1=ALU.add).then_inc(added, 1)


def connection_ffn(g, name):
    w0, w1, w2 = g.conn[:, 0:FF], g.conn[:, FF:FF + FT * FF], g.conn[:, FF + FT * FF:]
    with Stage(g, name) as st:
        ln = Norm(st, (0, 4), (1, 5))
        h = st.sb("h", [P, NB, FT, T])
        hidden, relu, out_ready, added = st.sem("hidden"), st.sem("relu"), st.sem("out_ready"), st.sem("added")
        with g.nc.Block() as block:
            @block.sync
            def _(sp):
                st.clear_spent(sp)

            @block.tensor
            def _(pe):
                ln.tensor(pe)
                for b in range(NB):
                    pe.wait_ge(ln.done, b + 1)
                    for f in range(FT):
                        mm = pe.matmul(g.ps[:, 4 * b + f, :], w0[:, f * P:(f + 1) * P], g.xn[:, b, :], start=True, stop=True)
                    mm.then_inc(hidden, 1)
                for b in range(NB):
                    pe.wait_ge(relu, b + 1)
                    for f in range(FT):
                        for k in range(FT):
                            mm = pe.matmul(g.ps[:, 4 * b + f, :], w1[:, k * FF + f * P:k * FF + (f + 1) * P], h[:, b, k, :],
                                           start=(k == 0), stop=(k == FT - 1))
                    mm.then_inc(hidden, 1)
                for b in range(NB):
                    pe.wait_ge(relu, NB + b + 1)
                    for k in range(FT):
                        mm = pe.matmul(g.ps[:, 4 * b, :], w2[:, k * P:(k + 1) * P], h[:, b, k, :], start=(k == 0), stop=(k == FT - 1))
                    mm.then_inc(out_ready, 1)

            @block.scalar
            def _(act):
                ln.scalar(act)
                for layer in range(2):
                    for b in range(NB):
                        act.wait_ge(hidden, layer * NB + b + 1)
                        act.activation(h[:, b, :, :], g.ps[:, 4 * b:4 * b + FT, :], ACT.Relu, scale=g.s2x[:, layer:layer + 1]).then_inc(relu, 1)

            @block.vector
            def _(dve):
                ln.vector(dve)
                for b in range(NB):
                    dve.wait_ge(out_ready, b + 1)
                    dve.scalar_tensor_tensor(out=g.xs[:, b, :], in0=g.ps[:, 4 * b, :], scalar=g.w("f1_s", 2, 1), in1=g.xs[:, b, :],
                                             op0=ALU.mult, op1=ALU.add).then_inc(added, 1)


def gated_ffn(g, name):
    NH = HID // P
    wg, wu, wd = g.gated[:, 0:HID], g.gated[:, HID:2 * HID], g.gated[:, 2 * HID:]
    with Stage(g, name) as st:
        ln = Norm(st, (0, 4), (1, 5))
        th = st.sb("th", [P, NB, NH, T])
        gate_ready, tanh_ready, half, up_ready = st.sem("gate_ready"), st.sem("tanh_ready"), st.sem("half"), st.sem("up_ready")
        act_ready, out_ready, added = st.sem("act_ready"), st.sem("out_ready"), st.sem("added")
        with g.nc.Block() as block:
            @block.sync
            def _(sp):
                st.clear_spent(sp)

            @block.tensor
            def _(pe):
                ln.tensor(pe)
                for b in range(NB):
                    pe.wait_ge(ln.done, b + 1)
                    for f in range(NH):
                        mm = pe.matmul(g.ps[:, 4 * b + f, :], wg[:, f * P:(f + 1) * P], g.xn[:, b, :], start=True, stop=True)
                    mm.then_inc(gate_ready, 1)
                for b in range(NB):
                    pe.wait_ge(half, b + 1)
                    for f in range(NH):
                        mm = pe.matmul(g.ps[:, 4 * b + f, :], wu[:, f * P:(f + 1) * P], g.xn[:, b, :], start=True, stop=True)
                    mm.then_inc(up_ready, 1)
                for b in range(NB):
                    pe.wait_ge(act_ready, b + 1)
                    for f in range(NH):
                        mm = pe.matmul(g.ps[:, 4 * b + 3, :], wd[:, f * P:(f + 1) * P], th[:, b, f, :], start=(f == 0), stop=(f == NH - 1))
                    mm.then_inc(out_ready, 1)

            @block.scalar
            def _(act):
                ln.scalar(act)
                for b in range(NB):
                    act.wait_ge(gate_ready, b + 1)
                    act.activation(th[:, b, :, :], g.ps[:, 4 * b:4 * b + NH, :], ACT.Tanh, scale=0.5).then_inc(tanh_ready, 1)

            @block.vector
            def _(dve):
                ln.vector(dve)
                for b in range(NB):
                    dve.wait_ge(tanh_ready, b + 1)
                    dve.scalar_tensor_tensor(out=th[:, b, :, :], in0=th[:, b, :, :], scalar=1.0, in1=g.ps[:, 4 * b:4 * b + NH, :],
                                             op0=ALU.add, op1=ALU.mult).then_inc(half, 1)
                for b in range(NB):
                    dve.wait_ge(up_ready, b + 1)
                    dve.wait_ge(half, b + 1)
                    dve.scalar_tensor_tensor(out=th[:, b, :, :], in0=th[:, b, :, :], scalar=0.5, in1=g.ps[:, 4 * b:4 * b + NH, :],
                                             op0=ALU.mult, op1=ALU.mult).then_inc(act_ready, 1)
                for b in range(NB):
                    dve.wait_ge(out_ready, b + 1)
                    dve.tensor_tensor(g.xs[:, b, :], g.xs[:, b, :], g.ps[:, 4 * b + 3, :], ALU.add).then_inc(added, 1)


def expert_ffn(g, name):
    NT = NB * KT
    with Stage(g, name) as st:
        ln = Norm(st, (4, 5), (6, 7))
        lg = st.sb("lg", [P, NT, E])
        hit = st.sb("hit", [P, NT, E])
        first = st.sb("first", [P, NT, E])
        second = st.sb("second", [P, NT, E])
        top = st.sb("top", [P, NT, 1])
        mask = st.sb("mask", [P, NT, E], BF16)
        masks = st.sb("masks", [P, NB, E, T])
        h = st.sb("h", [P, 2, FT, T])
        part = st.sb("part", [P, 2, T])
        gate_ready, picks, mask_ready = st.sem("gate_ready"), st.sem("picks"), st.sem("mask_ready")
        spread, mask_in = st.sem("spread"), st.sem("mask_in")
        hidden, relu, out_ready, masked, added = (st.sem(n) for n in ("hidden", "relu", "out_ready", "masked", "added"))
        w1 = st.sb("w1", [P, E, FF])
        w2 = st.sb("w2", [P, E, FF])
        expert_in = st.sem("expert_in")
        steps = NB * E
        gate = g.ps[:, 0, 0:NT * E].rearrange("p (t e) -> p t e", e=E)
        with g.nc.Block() as block:
            @block.sync
            def _(sp):
                st.clear_spent(sp)
                for e in range(E):
                    sp.dma_start(w1[:, e, :], g.experts[0, :, e * FF:(e + 1) * FF]).then_inc(expert_in, 16)
                    sp.dma_start(w2[:, e, :], g.experts[1, :, e * FF:(e + 1) * FF]).then_inc(expert_in, 16)
                    sp.wait_ge(expert_in, 32 * (e + 1))

            @block.tensor
            def _(pe):
                ln.tensor(pe)
                for b in range(NB):
                    pe.wait_ge(ln.done, b + 1)
                    for t in range(KT):
                        mm = pe.matmul(gate[:, b * KT + t, :], g.xn[:, b, t * P:(t + 1) * P], g.w("e2_gw"), start=True, stop=True)
                mm.then_inc(gate_ready, 1)

                def hidden_products(n):
                    b, e = n // E, n % E
                    if b == 0:
                        pe.wait_ge(expert_in, 32 * (e + 1))
                    for f in range(FT):
                        if n >= 1:
                            pe.wait_ge(relu, (n - 1) * FT + f + 1)
                        elif f == 0:
                            pe.wait_ge(picks, 1)
                        pe.matmul(g.ps[:, f, :], w1[:, e, f * P:(f + 1) * P], g.xn[:, b, :], start=True, stop=True).then_inc(hidden, 1)

                def results(n):
                    e = n % E
                    if n >= 2:
                        pe.wait_ge(masked, n - 1)
                    for f in range(FT):
                        pe.wait_ge(relu, n * FT + f + 1)
                        mm = pe.matmul(g.ps[:, 6 + n % 2, :], w2[:, e, f * P:(f + 1) * P], h[:, n % 2, f, :],
                                       start=(f == 0), stop=(f == FT - 1))
                    mm.then_inc(out_ready, 1)

                hidden_products(0)
                pe.wait_ge(mask_ready, 1)
                for n in range(steps):
                    if n >= 2:
                        pe.wait_ge(mask_in, n - 1)
                    b, e = n // E, n % E
                    for t in range(KT):
                        col = mask[:, b * KT + t, e:e + 1]
                        mm = pe.matmul(g.ps[:, 4 + n % 2, t * P:(t + 1) * P], widen(col, P), g.cb[:, 0:P], start=True, stop=True)
                    mm.then_inc(spread, 1)
                    if n + 1 < steps:
                        hidden_products(n + 1)
                    results(n)

            @block.scalar
            def _(act):
                ln.scalar(act)

                def relus(n):
                    for f in range(FT):
                        if n >= 2 and f == 0:
                            act.wait_ge(out_ready, n - 1)
                        act.wait_ge(hidden, n * FT + f + 1)
                        act.activation(h[:, n % 2, f, :], g.ps[:, f, :], ACT.Relu,
                                       bias=g.w("e2_b1", n % E * FT + f, 1)).then_inc(relu, 1)

                relus(0)
                for n in range(steps):
                    act.wait_ge(spread, n + 1)
                    act.activation(masks[:, n // E, n % E, :], g.ps[:, 4 + n % 2, :], ACT.Copy).then_inc(mask_in, 1)
                    if n + 1 < steps:
                        relus(n + 1)

            @block.vector
            def _(dve):
                ln.vector(dve)
                dve.wait_ge(gate_ready, 1)
                dve.tensor_tensor(lg[:, :, :], gate, bcast(g.w("e2_gb"), 1, NT), ALU.add).then_inc(picks, 1)
                rank = bcast(g.w("rank"), 1, NT)
                k = 1
                for pick in (first, second):
                    dve.wait_ge(picks, k)
                    dve.tensor_reduce(top[:, :, 0], lg[:, :, :], AX.X, ALU.max).then_inc(picks, 1)
                    dve.wait_ge(picks, k + 1)
                    dve.tensor_tensor(hit[:, :, :], lg[:, :, :], bcast(top[:, :, 0], 2, E), ALU.is_ge).then_inc(picks, 1)
                    dve.wait_ge(picks, k + 2)
                    dve.tensor_tensor(hit[:, :, :], hit[:, :, :], rank, ALU.mult).then_inc(picks, 1)
                    dve.wait_ge(picks, k + 3)
                    dve.tensor_reduce(top[:, :, 0], hit[:, :, :], AX.X, ALU.max).then_inc(picks, 1)
                    dve.wait_ge(picks, k + 4)
                    dve.tensor_tensor(pick[:, :, :], hit[:, :, :], bcast(top[:, :, 0], 2, E), ALU.is_equal).then_inc(picks, 1)
                    dve.wait_ge(picks, k + 5)
                    dve.scalar_tensor_tensor(out=lg[:, :, :], in0=pick[:, :, :], scalar=NEG, in1=lg[:, :, :],
                                             op0=ALU.mult, op1=ALU.add).then_inc(picks, 1)
                    k += 6
                dve.wait_ge(picks, k)
                dve.tensor_tensor(mask[:, :, :], first[:, :, :], second[:, :, :], ALU.add).then_inc(mask_ready, 1)
                for n in range(steps):
                    dve.wait_ge(out_ready, n + 1)
                    dve.wait_ge(mask_in, n + 1)
                    if n >= 2:
                        dve.wait_ge(added, n - 1)
                    dve.scalar_tensor_tensor(out=part[:, n % 2, :], in0=g.ps[:, 6 + n % 2, :], scalar=g.w("e2_b2", n % E, 1),
                                             in1=masks[:, n // E, n % E, :], op0=ALU.add, op1=ALU.mult).then_inc(masked, 1)

            @block.gpsimd
            def _(pool):
                pool.wait_ge(ln.done, NB)
                for n in range(steps):
                    pool.wait_ge(masked, n + 1)
                    if n >= 1:
                        pool.wait_ge(added, n)
                    b = n // E
                    pool.tensor_tensor(g.xs[:, b, :], g.xs[:, b, :], part[:, n % 2, :], ALU.add).then_inc(added, 1)


def single_head_attention(g, name):
    scale = P ** -0.5
    with Stage(g, name) as st:
        ln = Norm(st, (0, 1), (2, 3))
        q = st.sb("q", [P, NB, T])
        k = st.sb("k", [P, NB, T])
        v = st.sb("v", [P, NB, KT, P])
        s = st.sb("s", [P, 2, T])
        zero = st.sb("zero", [P, 2, T])
        pr = st.sb("pr", [P, 2, T])
        prt = st.sb("prt", [P, 2, KT, P])
        m = st.sb("m", [P, NB * KT])
        total = st.sb("total", [P, NB * KT])
        inv = st.sb("inv", [P, NB * KT])
        proj, proj_in = st.sem("proj"), st.sem("proj_in")
        score, scaled, max_ready, prob, norm = (st.sem(n) for n in ("score", "scaled", "max_ready", "prob", "norm"))
        turned, turned_in, out_ready, added = (st.sem(n) for n in ("turned", "turned_in", "out_ready", "added"))
        mask_steps, inverse = st.sem("mask_steps"), st.sem("inverse")
        with g.nc.Block() as block:
            @block.sync
            def _(sp):
                st.clear_spent(sp)

            @block.tensor
            def _(pe):
                ln.tensor(pe)
                for b in range(NB):
                    at = 4 - 4 * b
                    pe.wait_ge(ln.done, b + 1)
                    pe.matmul(g.ps[:, at, :], g.w("s2_wq"), g.xn[:, b, :], start=True, stop=True).then_inc(proj, 1)
                    pe.matmul(g.ps[:, at + 1, :], g.w("s2_wk"), g.xn[:, b, :], start=True, stop=True).then_inc(proj, 1)
                    for t in range(KT):
                        mm = pe.matmul(g.ps[:, at + 2, t * P:(t + 1) * P], g.xn[:, b, t * P:(t + 1) * P], g.w("s2_wv"), start=True, stop=True)
                    mm.then_inc(proj, 1)
                pe.wait_ge(proj_in, 3 * NB)

                def scores(n):
                    b, t = n // KT, n % KT
                    if n >= 2:
                        pe.wait_ge(scaled, n - 1)
                    pe.matmul(g.ps[:, n % 2, 0:(t + 1) * P], q[:, b, t * P:(t + 1) * P], k[:, b, 0:(t + 1) * P],
                              start=True, stop=True).then_inc(score, 1)

                scores(0)
                for n in range(NB * KT):
                    b, t = n // KT, n % KT
                    if n + 1 < NB * KT:
                        scores(n + 1)
                    pe.wait_ge(norm, n + 1)
                    if n >= 2:
                        pe.wait_ge(turned_in, n - 1)
                    for j in range(t + 1):
                        mm = pe.transpose(g.ps[:, 2 + n % 2, j * P:(j + 1) * P], pr[:, n % 2, j * P:(j + 1) * P], g.w("ident"))
                    mm.then_inc(turned, 1)
                    pe.wait_ge(turned_in, n + 1)
                    for j in range(t + 1):
                        mm = pe.matmul(g.ps[:, 4 + b, t * P:(t + 1) * P], v[:, b, j, :], prt[:, n % 2, j, :], start=(j == 0), stop=(j == t))
                    mm.then_inc(out_ready, 1)

            @block.scalar
            def _(act):
                ln.scalar(act)
                for b in range(NB):
                    at = 4 - 4 * b
                    act.wait_ge(proj, 3 * b + 3)
                    act.activation(q[:, b, :], g.ps[:, at, :], ACT.Copy).then_inc(proj_in, 1)
                    act.activation(k[:, b, :], g.ps[:, at + 1, :], ACT.Copy).then_inc(proj_in, 1)
                    act.activation(v[:, b, :, :], g.ps[:, at + 2, :].rearrange("p (t c) -> p t c", c=P), ACT.Copy).then_inc(proj_in, 1)
                for n in range(NB * KT):
                    t = n % KT
                    act.wait_ge(max_ready, 2 * n + 2)
                    if n >= 2:
                        act.wait_ge(turned, n - 1)
                    act.activation(pr[:, n % 2, 0:(t + 1) * P], s[:, n % 2, 0:(t + 1) * P], ACT.Exp, bias=m[:, n:n + 1],
                                   accum_out=total[:, n:n + 1]).then_inc(prob, 1)
                    if n >= 1:
                        act.wait_ge(turned, n)
                        if n >= 3:
                            act.wait_ge(out_ready, n - 2)
                        w = (n - 1) % KT + 1
                        act.activation(prt[:, (n - 1) % 2, 0:w, :], g.ps[:, 2 + (n - 1) % 2, 0:w * P].rearrange("p (t c) -> p t c", c=P),
                                       ACT.Copy).then_inc(turned_in, 1)
                n = NB * KT
                act.wait_ge(turned, n)
                act.wait_ge(out_ready, n - 2)
                act.activation(prt[:, (n - 1) % 2, :, :], g.ps[:, 2 + (n - 1) % 2, :].rearrange("p (t c) -> p t c", c=P),
                               ACT.Copy).then_inc(turned_in, 1)

            @block.vector
            def _(dve):
                ln.vector(dve)
                for n in range(NB * KT):
                    b, t = n // KT, n % KT
                    w = (t + 1) * P
                    dve.wait_ge(score, n + 1)
                    if n >= 2:
                        dve.wait_ge(prob, n - 1)
                    dve.tensor_scalar(s[:, n % 2, 0:w], g.ps[:, n % 2, 0:w], scale, None, ALU.mult).then_inc(scaled, 1)
                    dve.wait_ge(scaled, n + 1)
                    dve.tensor_tensor(s[:, n % 2, w - P:w], s[:, n % 2, w - P:w], g.w("tri"), ALU.mult).then_inc(mask_steps, 1)
                    dve.wait_ge(mask_steps, 3 * n + 1)
                    dve.tensor_scalar(zero[:, n % 2, 0:w], s[:, n % 2, 0:w], 0.0, None, ALU.is_equal).then_inc(mask_steps, 1)
                    dve.wait_ge(mask_steps, 3 * n + 2)
                    dve.scalar_tensor_tensor(out=s[:, n % 2, 0:w], in0=zero[:, n % 2, 0:w], scalar=NEG, in1=s[:, n % 2, 0:w],
                                             op0=ALU.mult, op1=ALU.add).then_inc(mask_steps, 1)
                    dve.wait_ge(mask_steps, 3 * n + 3)
                    dve.tensor_reduce(m[:, n:n + 1], s[:, n % 2, 0:w], AX.X, ALU.max).then_inc(max_ready, 1)
                    dve.wait_ge(max_ready, 2 * n + 1)
                    dve.tensor_scalar(m[:, n:n + 1], m[:, n:n + 1], -1.0, None, ALU.mult).then_inc(max_ready, 1)
                    dve.wait_ge(prob, n + 1)
                    dve.reciprocal(inv[:, n:n + 1], total[:, n:n + 1]).then_inc(inverse, 1)
                    dve.wait_ge(inverse, n + 1)
                    dve.tensor_scalar(pr[:, n % 2, 0:w], pr[:, n % 2, 0:w], inv[:, n:n + 1], None, ALU.mult).then_inc(norm, 1)
                for b in range(NB):
                    dve.wait_ge(out_ready, (b + 1) * KT)
                    dve.tensor_tensor(g.xs[:, b, :], g.xs[:, b, :], g.ps[:, 4 + b, :], ALU.add).then_inc(added, 1)


def linear_attention(g, name):
    NT = NB * KT
    with Stage(g, name) as st:
        ln = Norm(st, (0, 1), (2, 3))
        q = st.sb("q", [P, NB, T])
        k = st.sb("k", [P, NB, T])
        kt = st.sb("kt", [P, NB, KT, P])
        v = st.sb("v", [P, NB, KT, P])
        vpad = st.sb("vpad", [P, NT, H, 32])
        e = st.sb("e", [P, NB, 4, T])
        km = st.sb("km", [P, NB, 4, T])
        at = st.sb("at", [P, 2, H, P])
        state = st.sb("state", [P, NT, P])
        z = st.sb("z", [P, NB, T])
        o = st.sb("o", [P, NB, T])
        proj, ex, low, feat, rest_in = (st.sem(n) for n in ("proj", "ex", "low", "feat", "rest_in"))
        km_ready, zero, v_ready = st.sem("km_ready"), st.sem("zero"), st.sem("v_ready")
        cum, cum_in, dot, z_steps = (st.sem(n) for n in ("cum", "cum_in", "dot", "z_steps"))
        kv, kv_in, att, att_in, num, out_in, out_ready, added = (
            st.sem(n) for n in ("kv", "kv_in", "att", "att_in", "num", "out_in", "out_ready", "added"))
        with g.nc.Block() as block:
            @block.sync
            def _(sp):
                st.clear_spent(sp)

            @block.tensor
            def _(pe):
                ln.tensor(pe)
                for b in range(NB):
                    pe.wait_ge(ln.done, b + 1)
                    if b >= 1:
                        pe.wait_ge(feat, 3 * b)
                        pe.wait_ge(v_ready, b)
                    pe.matmul(g.ps[:, 4, :], g.w("l1_wq"), g.xn[:, b, :], start=True, stop=True)
                    pe.matmul(g.ps[:, 5, :], g.w("l1_wk"), g.xn[:, b, :], start=True, stop=True)
                    for t in range(KT):
                        pe.matmul(g.ps[:, 6, t * P:(t + 1) * P], g.xn[:, b, t * P:(t + 1) * P], g.w("l1_wk"), start=True, stop=True)
                        mm = pe.matmul(g.ps[:, 7, t * P:(t + 1) * P], g.xn[:, b, t * P:(t + 1) * P], g.w("l1_wv"), start=True, stop=True)
                    mm.then_inc(proj, 1)
                for b in range(NB):
                    pe.wait_ge(feat, 3 * NB)
                    pe.matmul(g.ps[:, b, :], g.w("head_cum"), k[:, b, :], start=True, stop=True).then_inc(cum, 1)
                for b in range(NB):
                    pe.wait_ge(cum_in, b + 1)
                    pe.matmul(g.ps[:, b, :], g.w("head_sum"), z[:, b, :], start=True, stop=True).then_inc(dot, 1)
                for n in range(NT):
                    b, t = n // KT, n % KT
                    if t == KT - 1:
                        continue
                    if n - b >= 2:
                        pe.wait_ge(kv_in, n - b - 1)
                    pe.wait_ge(v_ready, NB)
                    for j in range(t + 1):
                        mm = pe.matmul(g.ps[:, 2 + (n - b) % 2, 0:P], kt[:, b, j, :], v[:, b, j, :], start=(j == 0), stop=(j == t))
                    mm.then_inc(kv, 1)
                pe.wait_ge(kv_in, NT - NB)
                pe.wait_ge(zero, 2)
                pe.wait_ge(km_ready, 4)
                pe.wait_ge(z_steps, 2 * NB)

                def tile_scores(i):
                    b, t = i // KT, i % KT
                    for r in range(4):
                        n = 4 * i + r
                        if n >= 2:
                            pe.wait_ge(att_in, n - 1)
                        rows = slice(32 * r, 32 * r + 32)
                        for c in range(4):
                            mm = pe.matmul(g.ps[:, 4 + n % 2, c * P:(c + 1) * P], km[rows, b, c, t * P:(t + 1) * P],
                                           q[rows, b, t * P:(t + 1) * P], start=True, stop=True)
                        mm.then_inc(att, 1)

                tile_scores(0)
                for i in range(NT):
                    b, t = i // KT, i % KT
                    if i + 1 < NT:
                        tile_scores(i + 1)
                    pe.wait_ge(att_in, 4 * i + 4)
                    if i >= 2:
                        pe.wait_ge(out_in, i - 1)
                    dst = g.ps[:, 6 + i % 2, 0:P]
                    if t > 0:
                        pe.matmul(dst, state[:, i, :], q[:, b, t * P:(t + 1) * P], start=True, stop=False, skip_group_check=True)
                    for c in range(4):
                        for r in range(4):
                            mm = pe.matmul(dst[32 * r:32 * r + 32, :], vpad[:, i, 4 * r + c, :], at[:, i % 2, 4 * r + c, :],
                                           start=(c == 0 and t == 0), stop=(c == 3), skip_group_check=True)
                    mm.then_inc(num, 1)
                for b in range(NB):
                    pe.wait_ge(out_in, (b + 1) * KT)
                    pe.matmul(g.ps[:, b, :], g.w("l1_wo"), o[:, b, :], start=True, stop=True).then_inc(out_ready, 1)

            @block.scalar
            def _(act):
                ln.scalar(act)
                for b in range(NB):
                    for j in range(3):
                        act.wait_ge(low, 3 * b + j + 1)
                        act.activation(e[:, b, j, :], e[:, b, j, :], ACT.Exp).then_inc(ex, 1)
                    act.wait_ge(proj, b + 1)
                    act.activation(v[:, b, :, :], g.ps[:, 7, :].rearrange("p (t c) -> p t c", c=P), ACT.Copy).then_inc(v_ready, 1)

            @block.gpsimd
            def _(pool):
                pool.memset(vpad[:, :, :, :], 0.0).then_inc(zero, 1)
                pool.wait_ge(zero, 1)
                pool.wait_ge(v_ready, NB)
                for c in range(4):
                    for i in range(NT):
                        ins = pool.tensor_copy(vpad[:, i, c:H:4, 8 * c:8 * c + 8],
                                               v[:, i // KT, i % KT, :].rearrange("p (r c f) -> p r c f", r=4, c=4)[:, :, c, :])
                ins.then_inc(zero, 1)

            @block.vector
            def _(dve):
                ln.vector(dve)
                dst = (q, k, kt)
                for b in range(NB):
                    dve.wait_ge(proj, b + 1)
                    for j in range(3):
                        dve.tensor_scalar(e[:, b, j, :], g.ps[:, 4 + j, :], 0.0, None, ALU.min).then_inc(low, 1)
                    for j in range(3):
                        dve.wait_ge(ex, 3 * b + j + 1)
                        out = dst[j][:, b, :] if j < 2 else kt[:, b, :, :].rearrange("p t c -> p (t c)")
                        dve.scalar_tensor_tensor(out=out, in0=g.ps[:, 4 + j, :], scalar=0.0, in1=e[:, b, j, :],
                                                 op0=ALU.max, op1=ALU.add).then_inc(feat, 1)
                for b in range(NB):
                    dve.wait_ge(cum, b + 1)
                    dve.wait_ge(feat, 3 * NB)
                    dve.tensor_tensor(z[:, b, :], q[:, b, :], g.ps[:, b, :], ALU.mult).then_inc(cum_in, 1)
                for b in range(NB):
                    dve.wait_ge(dot, b + 1)
                    dve.tensor_scalar(z[:, b, :], g.ps[:, b, :], 1e-6, None, ALU.add).then_inc(z_steps, 1)
                    dve.wait_ge(z_steps, 2 * b + 1)
                    dve.reciprocal(z[:, b, :], z[:, b, :]).then_inc(z_steps, 1)
                for n in range(NT - NB):
                    b, t = n // (KT - 1), n % (KT - 1)
                    dve.wait_ge(kv, n + 1)
                    dve.tensor_tensor(state[:, b * KT + t + 1, :], g.ps[:, 2 + n % 2, 0:P], g.w("head_sum"), ALU.mult).then_inc(kv_in, 1)
                dve.wait_ge(z_steps, 2 * NB)
                for c in range(4):
                    dve.tensor_scalar(km[:, :, c, :], k[:, :, :], g.w("head_of", c, 1), None, ALU.mult).then_inc(km_ready, 1)

                def finish(i):
                    b, t = i // KT, i % KT
                    dve.wait_ge(num, i + 1)
                    dve.tensor_tensor(o[:, b, t * P:(t + 1) * P], g.ps[:, 6 + i % 2, 0:P], z[:, b, t * P:(t + 1) * P], ALU.mult).then_inc(out_in, 1)

                for n in range(4 * NT):
                    i, r = n // 4, n % 4
                    if r == 0 and i >= 2:
                        finish(i - 2)
                    dve.wait_ge(att, n + 1)
                    dve.tensor_tensor(at[:, i % 2, 4 * r:4 * r + 4, :], g.ps[:, 4 + n % 2, :].rearrange("p (r c) -> p r c", c=P),
                                      bcast(g.w("tri_t"), 1, 4), ALU.mult).then_inc(att_in, 1)
                finish(NT - 2)
                finish(NT - 1)
                for b in range(NB):
                    dve.wait_ge(out_ready, b + 1)
                    dve.scalar_tensor_tensor(out=g.xs[:, b, :], in0=g.ps[:, b, :], scalar=g.w("l1_bo"), in1=g.xs[:, b, :],
                                             op0=ALU.add, op1=ALU.add).then_inc(added, 1)


def mamba(g, name, w, variant):
    KP = 96 + (8 if variant == 0 else 1)
    st = Stage(g, name)
    with st:
        ln = Norm(st, (0, 1), (2, 3))
        tm = st.sb("tm", [P, 2, T])
        up = st.sb("up", [P, 2, T + 3])
        u = st.sb("u", [P, NB, 2, T])
        gate = st.sb("gate", [P, NB, 2, T])
        dt = st.sb("dt", [P, NB, 2, T])
        du = st.sb("du", [P, NB, 2, T])
        da = st.sb("da", [P, 2, 2, T])
        db = st.sb("db", [P, 2, 2, T])
        bs = st.sb("bs", [P, 2, T])
        hs = st.sb("hs", [P, 2, 2, T])
        hc = st.sb("hc", [P, 2, 2, T])
        dbc = st.sb("dbc", [KP, T])
        rest = st.sb("rest", [96, T])
        cut = st.sb("cut", [96, T], BF16)
        bc = st.sb("bc", [96, NB, T], BF16)
        y = st.sb("y", [P, NB, 2, T])
        pre, rms_sq, rms_ms, rms_log, rms_r, rms_out = (st.sem(n) for n in ("pre", "rms_sq", "rms_ms", "rms_log", "rms_r", "rms_out"))
        uz, uz_in, conv, conv_tanh, u_ready, z_tanh, gate_ready = (
            st.sem(n) for n in ("uz", "uz_in", "conv", "conv_tanh", "u_ready", "z_tanh", "gate_ready"))
        xp, xp_in, split, dtp, dt_steps, dt_exp, dt_log, dt_ready = (
            st.sem(n) for n in ("xp", "xp_in", "split", "dtp", "dt_steps", "dt_exp", "dt_log", "dt_ready"))
        zeros, decay, b_row, c_row, b_in, input_ready, scanned, weighed, summed = (
            st.sem(n) for n in ("zeros", "decay", "b_row", "c_row", "b_in", "input_ready", "scanned", "weighed", "summed"))
        y_steps, y_ready, out_ready, added = (st.sem(n) for n in ("y_steps", "y_ready", "out_ready", "added"))
        mlp_h, mlp_in, resid, u_half, dt_sum, split_steps, pre_c, rms_mid, dt_abs = (
            st.sem(n) for n in ("mlp_h", "mlp_in", "resid", "u_half", "dt_sum", "split_steps", "pre_c", "rms_mid", "dt_abs"))
        steps = NB * NS

        def rms_sum(pe, base):
            for b in range(NB):
                pe.wait_ge(rms_sq, base * NB + b + 1)
                pe.matmul(g.ps[:, b, :], g.w("mean_mat"), ln.sq[:, b, :], start=True, stop=True).then_inc(rms_ms, 1)

        def rms_scalar(act, base, src, eps):
            for b in range(NB):
                act.activation(ln.sq[:, b, :], src[:, b, :], ACT.Square).then_inc(rms_sq, 1)
            for b in range(NB):
                act.wait_ge(rms_ms, base * NB + b + 1)
                act.activation(ln.sq[:, b, :], g.ps[:, b, :], ACT.Ln, bias=g.w(eps)).then_inc(rms_log, 1)
                act.wait_ge(rms_log, base * NB + b + 1)
                act.activation(ln.sq[:, b, :], ln.sq[:, b, :], ACT.Exp, scale=-0.5).then_inc(rms_r, 1)

        with g.nc.Block() as block:
            @block.sync
            def _(sp):
                st.clear_spent(sp)

            @block.tensor
            def _(pe):
                ln.tensor(pe)
                if variant == 1:
                    for b in range(NB):
                        pe.wait_ge(ln.done, b + 1)
                        pe.matmul(g.ps[:, 4 + b, :], g.w("mean_mat"), g.xn[:, b, :], start=True, stop=True).then_inc(pre, 1)
                rms_sum(pe, 0)
                for b in range(NB):
                    pe.wait_ge(rms_out, b + 1)
                    if b == 0:
                        pe.wait_ge(rms_out, NB)
                    pe.wait_ge(rms_r, NB)
                    if b >= 1:
                        pe.wait_ge(uz_in, b)
                        pe.wait_ge(gate_ready, b)
                    for f in range(4):
                        mm = pe.matmul(g.ps[:, f, :], g.w(w + "_in", f * P, P), y[:, b, 0, :], start=True, stop=True)
                    mm.then_inc(uz, 1)
                    pe.wait_ge(u_ready, b + 1)
                    for k in range(2):
                        mm = pe.matmul(g.ps[0:KP, 4, :], g.w(w + "_xp", k * KP, KP), u[:, b, k, :], start=(k == 0), stop=(k == 1))
                    mm.then_inc(xp, 1)
                    pe.wait_ge(xp_in, b + 1)
                    if b >= 1:
                        pe.wait_ge(dt_abs, 2 * b)
                    for k in range(2):
                        wt = g.w(w + "_dtw", k * P, P)[96:KP, :]
                        mm = pe.matmul(g.ps[:, 6 + k, :], wt, dbc[96:KP, :], start=True, stop=True)
                    mm.then_inc(dtp, 1)

                def rows(n):
                    b, s = n // NS, n % NS
                    if n >= 2:
                        pe.wait_ge(b_in, n - 1)
                        pe.wait_ge(weighed, n - 1)
                    pe.matmul(g.ps[:, 2 + n % 2, :], widen(g.cb[0:96, 384 + s:385 + s], P), bc[:, b, :], start=True, stop=True).then_inc(b_row, 1)
                    pe.matmul(g.ps[:, 4 + n % 2, :], widen(g.cb[0:96, 400 + s:401 + s], P), bc[:, b, :], start=True, stop=True).then_inc(c_row, 1)

                pe.wait_ge(split, NB)
                pe.wait_ge(gate_ready, NB)
                pe.wait_ge(dt_ready, NB)
                rows(0)
                rows(1)
                for n in range(steps):
                    b, s = n // NS, n % NS
                    pe.wait_ge(weighed, n + 1)
                    if s == 0 and b >= 1:
                        pe.wait_ge(y_steps, b)
                    for k in range(2):
                        mm = pe.matmul(g.ps[:, k, :], g.w("ident"), hc[:, n % 2, k, :], start=(s == 0), stop=(s == NS - 1))
                    mm.then_inc(summed, 1)
                    if n + 2 < steps:
                        rows(n + 2)
                for b in range(NB):
                    pe.wait_ge(y_ready, b + 1)
                    for k in range(2):
                        mm = pe.matmul(g.ps[:, 6 + b, :], g.w(w + "_out", k * P, P), y[:, b, k, :], start=(k == 0), stop=(k == 1))
                    mm.then_inc(out_ready, 1)
                if variant == 0:
                    rms_sum(pe, 1)
                    for b in range(NB):
                        pe.wait_ge(rms_out, NB + b + 1)
                        pe.wait_ge(rms_out, 2 * NB)
                        for f in range(2):
                            mm = pe.matmul(g.ps[:, 2 * b + f, :], g.w("m0_fc1", f * P, P), y[:, b, 0, :], start=True, stop=True)
                        mm.then_inc(mlp_h, 1)
                    for b in range(NB):
                        pe.wait_ge(mlp_in, 2 * b + 2)
                        for f in range(2):
                            for k in range(2):
                                mm = pe.matmul(g.ps[:, 2 * b + f, :], g.w("m0_fc2", k * 2 * P + f * P, P), u[:, b, k, :], start=(k == 0), stop=(k == 1))
                        mm.then_inc(mlp_h, 1)
                    for b in range(NB):
                        pe.wait_ge(mlp_in, 2 * NB + 2 * b + 2)
                        for k in range(2):
                            mm = pe.matmul(g.ps[:, 4 + b, :], g.w("m0_fc3", k * P, P), du[:, b, k, :], start=(k == 0), stop=(k == 1))
                        mm.then_inc(mlp_h, 1)

            @block.scalar
            def _(act):
                ln.scalar(act)
                if variant == 0:
                    act.wait_ge(ln.done, NB)
                    rms_scalar(act, 0, g.xn, "eps6")
                else:
                    act.wait_ge(pre_c, NB)
                    rms_scalar(act, 0, ln.xc, "eps5")
                for b in range(NB):
                    act.wait_ge(uz, b + 1)
                    act.wait_ge(zeros, 1)
                    if b >= 1:
                        act.wait_ge(conv, 8 * b)
                    act.activation(up[:, :, 3:], g.ps[:, 0:2, :], ACT.Copy).then_inc(uz_in, 1)
                    if b >= 1:
                        act.wait_ge(gate_ready, b)
                    act.activation(gate[:, b, :, :], g.ps[:, 2:4, :], ACT.Tanh, scale=0.5).then_inc(z_tanh, 1)
                    act.wait_ge(conv, 8 * b + 8)
                    act.activation(u[:, b, :, :], tm[:, 0:2, :], ACT.Tanh, scale=0.5).then_inc(conv_tanh, 1)
                    act.wait_ge(dt_steps, 2 * b + 2)
                    for k in range(2):
                        act.activation(du[:, b, k, :], g.ps[:, 6 + k, :], ACT.Abs, bias=g.w(w + "_dtb", k, 1)).then_inc(dt_abs, 1)
                    act.wait_ge(dt_abs, 2 * b + 2)
                    act.activation(du[:, b, :, :], du[:, b, :, :], ACT.Exp, scale=-1.0).then_inc(dt_exp, 1)
                    act.wait_ge(dt_exp, b + 1)
                    act.activation(du[:, b, :, :], du[:, b, :, :], ACT.Ln, bias=1.0).then_inc(dt_log, 1)

                def decays(n):
                    b, s = n // NS, n % NS
                    if n >= 2:
                        act.wait_ge(scanned, n - 1)
                    act.wait_ge(dt_ready, b + 1)
                    for k in range(2):
                        ins = act.activation(da[:, n % 2, k, 1:], dt[:, b, k, 1:], ACT.Exp, scale=g.A[:, variant, k * NS + s:k * NS + s + 1])
                    ins.then_inc(decay, 1)

                act.wait_ge(zeros, 2)
                decays(0)
                for n in range(steps):
                    act.wait_ge(b_row, n + 1)
                    if n >= 2:
                        act.wait_ge(input_ready, n - 1)
                    act.activation(bs[:, n % 2, :], g.ps[:, 2 + n % 2, :], ACT.Copy).then_inc(b_in, 1)
                    if n + 1 < steps:
                        decays(n + 1)
                if variant == 0:
                    act.wait_ge(added, NB)
                    rms_scalar(act, 1, ln.xc, "eps6")
                    for layer, (bias, dst) in enumerate((("m0_fc1b", u), ("m0_fc2b", du))):
                        for b in range(NB):
                            act.wait_ge(mlp_h, layer * NB + b + 1)
                            for f in range(2):
                                act.activation(dst[:, b, f, :], g.ps[:, 2 * b + f, :], ACT.Relu, bias=g.w(bias, f, 1)).then_inc(mlp_in, 1)

            @block.gpsimd
            def _(pool):
                pool.memset(up[:, :, 0:3], 0.0).then_inc(zeros, 1)
                pool.memset(da[:, :, :, 0:1], 0.0).then_inc(zeros, 1)
                for n in range(steps):
                    b = n // NS
                    pool.wait_ge(b_in, n + 1)
                    pool.wait_ge(dt_ready, b + 1)
                    if n >= 2:
                        pool.wait_ge(scanned, n - 1)
                    pool.tensor_tensor(db[:, n % 2, :, :], du[:, b, :, :], bcast(bs[:, n % 2, :], 1, 2), ALU.mult).then_inc(input_ready, 1)

            @block.vector
            def _(dve):
                ln.vector(dve)
                if variant == 1:
                    for b in range(NB):
                        dve.wait_ge(pre, b + 1)
                        dve.wait_ge(ln.done, NB)
                        dve.tensor_tensor(ln.xc[:, b, :], g.xn[:, b, :], g.ps[:, 4 + b, :], ALU.subtract).then_inc(pre_c, 1)
                for b in range(NB):
                    dve.wait_ge(rms_r, b + 1)
                    if variant == 0:
                        dve.wait_ge(ln.done, NB)
                        dve.scalar_tensor_tensor(out=y[:, b, 0, :], in0=g.xn[:, b, :], scalar=g.w("m0_rms1"), in1=ln.sq[:, b, :],
                                                 op0=ALU.mult, op1=ALU.mult).then_inc(rms_out, 1)
                    else:
                        dve.scalar_tensor_tensor(out=y[:, b, 1, :], in0=ln.xc[:, b, :], scalar=g.w("m3_nw"), in1=ln.sq[:, b, :],
                                                 op0=ALU.mult, op1=ALU.mult).then_inc(rms_mid, 1)
                        dve.wait_ge(rms_mid, b + 1)
                        dve.tensor_scalar(y[:, b, 0, :], y[:, b, 1, :], g.w("m3_nb"), None, ALU.add).then_inc(rms_out, 1)
                for b in range(NB):
                    dve.wait_ge(uz_in, b + 1)
                    if b >= 1:
                        dve.wait_ge(u_ready, b)
                    for k in range(2):
                        tap = lambda j: g.w(w + "_cw", k * 4 + j, 1)
                        dve.tensor_scalar(tm[:, k, :], up[:, k, 0:T], tap(0), g.w(w + "_cb", k, 1), ALU.mult, ALU.add).then_inc(conv, 1)
                        for j in range(1, 4):
                            dve.wait_ge(conv, 8 * b + 4 * k + j)
                            dve.scalar_tensor_tensor(out=tm[:, k, :], in0=up[:, k, j:j + T], scalar=tap(j), in1=tm[:, k, :],
                                                     op0=ALU.mult, op1=ALU.add).then_inc(conv, 1)
                    dve.wait_ge(z_tanh, b + 1)
                    dve.scalar_tensor_tensor(out=gate[:, b, :, :], in0=gate[:, b, :, :], scalar=1.0, in1=g.ps[:, 2:4, :],
                                             op0=ALU.add, op1=ALU.mult).then_inc(gate_ready, 1)
                    dve.wait_ge(conv_tanh, b + 1)
                    dve.scalar_tensor_tensor(out=u[:, b, :, :], in0=u[:, b, :, :], scalar=1.0, in1=tm[:, 0:2, :],
                                             op0=ALU.add, op1=ALU.mult).then_inc(u_half, 1)
                    dve.wait_ge(u_half, b + 1)
                    dve.tensor_scalar(u[:, b, :, :], u[:, b, :, :], 0.5, None, ALU.mult).then_inc(u_ready, 1)
                    dve.wait_ge(xp, b + 1)
                    if b >= 1:
                        dve.wait_ge(dtp, b)
                        dve.wait_ge(split, b)
                    dve.tensor_copy(dbc[:, :], g.ps[0:KP, 4, :]).then_inc(xp_in, 1)
                    for m in range(3):
                        src = dbc if m == 0 else rest
                        dve.wait_ge(xp_in, b + 1)
                        if m:
                            dve.wait_ge(split_steps, 2 * (2 * b + m))
                        ins = dve.tensor_copy(bc[32 * m:32 * m + 32, b, :], src[32 * m:32 * m + 32, :])
                        if m == 2:
                            ins.then_inc(split, 1)
                            continue
                        dve.tensor_copy(cut[:, :], src[0:96, :]).then_inc(split_steps, 1)
                        dve.wait_ge(split_steps, 2 * (2 * b + m) + 1)
                        dve.tensor_tensor(rest[:, :], src[0:96, :], cut[:, :], ALU.subtract).then_inc(split_steps, 1)
                    dve.wait_ge(dtp, b + 1)
                    for k in range(2):
                        bias = g.w(w + "_dtb", k, 1)
                        dve.tensor_scalar(dt[:, b, k, :], g.ps[:, 6 + k, :], bias, 0.0, ALU.add, ALU.max).then_inc(dt_steps, 1)
                    dve.wait_ge(dt_log, b + 1)
                    dve.tensor_tensor(dt[:, b, :, :], dt[:, b, :, :], du[:, b, :, :], ALU.add).then_inc(dt_sum, 1)
                    dve.wait_ge(dt_sum, b + 1)
                    dve.tensor_tensor(du[:, b, :, :], dt[:, b, :, :], u[:, b, :, :], ALU.mult).then_inc(dt_ready, 1)
                for n in range(steps):
                    b, s = n // NS, n % NS
                    dve.wait_ge(decay, n + 1)
                    dve.wait_ge(input_ready, n + 1)
                    if n >= 2:
                        dve.wait_ge(weighed, n - 1)
                    flat = lambda tile: tile[:, n % 2, :, :].rearrange("p k t -> p (k t)")
                    dve.tensor_tensor_scan(flat(hs), flat(da), flat(db), 0.0, ALU.mult, ALU.add).then_inc(scanned, 1)
                    dve.wait_ge(scanned, n + 1)
                    dve.wait_ge(c_row, n + 1)
                    if n >= 2:
                        dve.wait_ge(summed, n - 1)
                    dve.tensor_tensor(hc[:, n % 2, :, :], hs[:, n % 2, :, :], bcast(g.ps[:, 4 + n % 2, :], 1, 2), ALU.mult).then_inc(weighed, 1)
                    if s == NS - 1:
                        dve.wait_ge(summed, n + 1)
                        for k in range(2):
                            ins = dve.scalar_tensor_tensor(out=y[:, b, k, :], in0=u[:, b, k, :], scalar=g.w(w + "_d", k, 1), in1=g.ps[:, k, :],
                                                           op0=ALU.mult, op1=ALU.add)
                        ins.then_inc(y_steps, 1)
                        dve.wait_ge(y_steps, b + 1)
                        dve.scalar_tensor_tensor(out=y[:, b, :, :], in0=y[:, b, :, :], scalar=0.5, in1=gate[:, b, :, :],
                                                 op0=ALU.mult, op1=ALU.mult).then_inc(y_ready, 1)
                if variant == 0:
                    for b in range(NB):
                        dve.wait_ge(out_ready, b + 1)
                        dve.tensor_tensor(ln.xc[:, b, :], g.xn[:, b, :], g.ps[:, 6 + b, :], ALU.add).then_inc(added, 1)
                    for b in range(NB):
                        dve.wait_ge(rms_r, NB + b + 1)
                        dve.wait_ge(added, NB)
                        dve.scalar_tensor_tensor(out=y[:, b, 0, :], in0=ln.xc[:, b, :], scalar=g.w("m0_rms2"), in1=ln.sq[:, b, :],
                                                 op0=ALU.mult, op1=ALU.mult).then_inc(rms_out, 1)
                        dve.tensor_tensor(g.xs[:, b, :], g.xs[:, b, :], ln.xc[:, b, :], ALU.add).then_inc(resid, 1)
                    for b in range(NB):
                        dve.wait_ge(mlp_h, 2 * NB + b + 1)
                        dve.wait_ge(resid, NB)
                        dve.scalar_tensor_tensor(out=g.xs[:, b, :], in0=g.ps[:, 4 + b, :], scalar=g.w("m0_fc3b"), in1=g.xs[:, b, :],
                                                 op0=ALU.add, op1=ALU.add).then_inc(resid, 1)
                else:
                    for b in range(NB):
                        dve.wait_ge(out_ready, b + 1)
                        dve.tensor_tensor(ln.sq[:, b, :], g.xn[:, b, :], g.ps[:, 6 + b, :], ALU.add).then_inc(added, 1)
                        dve.wait_ge(added, b + 1)
                        dve.tensor_tensor(g.xs[:, b, :], g.xs[:, b, :], ln.sq[:, b, :], ALU.add).then_inc(resid, 1)


Q_PART = (0, 0, 1, 1, 0, 2)
K_PART = (0, 1, 0, 1, 2, 0)
ROWS = len(Q_PART) * DH


def narrow_attention(g, name, w, causal, scale):
    UN = NB * 4
    with Stage(g, name) as st:
        ln = Norm(st, (0, 1), (2, 3))
        qs = st.sb("qs", [ROWS + 3, NB, 4, 4, T], BF16)
        ks = st.sb("ks", [ROWS + 3, NB, 4, 4, T], BF16)
        cut = st.sb("cut", [P, 3, 2, T], BF16)
        val = ln.xc
        v = st.sb("v", [P, NB, KT, P])
        vpad = st.sb("vpad", [P, NB, KT, H, 32])
        pt = st.sb("pt", [P, 3, 4, T])
        mx = st.sb("mx", [P, UN, 16])
        mt = st.sb("mt", [16, 2, P])
        mcut = st.sb("mcut", [16, 2, 3, P], BF16)
        inv = g.xn[:, 0, :]
        at = ln.sq
        proj, proj_in, cuts, cuts_act, stacked, ones_in, v_in, zero, vpad_ready = (
            st.sem(n) for n in ("proj", "proj_in", "cuts", "cuts_act", "stacked", "ones_in", "v_in", "zero", "vpad_ready"))
        top, top_in, m_steps, m_rows = (st.sem(n) for n in ("top", "top_in", "m_steps", "m_rows"))
        score, prob, pv, inv_ready, at_ready, at_bias, out_ready, added = (
            st.sem(n) for n in ("score", "prob", "pv", "inv_ready", "at_ready", "at_bias", "out_ready", "added"))
        parted = st.sem("parted")
        mask_qk, mask_kq = g.cb[:, P:2 * P], g.cb[:, 2 * P:3 * P]
        eye = g.cb[:, 0:P]

        def span(t):
            return (t + 1) * P if causal else T

        def first(k):
            return k * P if causal else 0

        with g.nc.Block() as block:
            @block.sync
            def _(sp):
                st.clear_spent(sp)
                for b in range(NB):
                    sp.wait_ge(cuts, 5 * b + 5)
                    sp.dma_start(g.parts_dram[b], cut[:, :, :, :]).then_inc(parted, 16)
                    sp.wait_ge(parted, 16 * (b + 1))
                sp.wait_ge(ones_in, 1)
                for b in range(NB):
                    for j in range(len(Q_PART)):
                        for x, part, dst in ((0, Q_PART[j], qs), (1, K_PART[j], ks)):
                            for i in range(4):
                                src = g.parts_dram[b, :, part, x, :].rearrange("(r i f) t -> i f r t", r=4, i=4)[i]
                                sp.dma_start(dst[DH * j:DH * j + DH, b, i, :, :], src).then_inc(stacked, 16)
                for u in range(UN):
                    b, i = u // 4, u % 4
                    sp.wait_ge(m_steps, 6 * u + 6)
                    for p in range(3):
                        sp.dma_start(qs[ROWS + p:ROWS + p + 1, b, i, :, :].rearrange("o r (t c) -> o (r t) c", c=P),
                                     mcut[:, u % 2, p, :]).then_inc(m_rows, 16)
                    sp.wait_ge(m_rows, 48 * (u + 1))

            @block.tensor
            def _(pe):
                ln.tensor(pe)
                for b in range(NB):
                    pe.wait_ge(ln.done, NB)
                    if b >= 1:
                        pe.wait_ge(proj_in, 2 * b)
                        pe.wait_ge(v_in, b)
                    pe.matmul(g.ps[:, 0, :], g.w(w + "_wq"), g.xn[:, b, :], start=True, stop=True)
                    pe.matmul(g.ps[:, 1, :], g.w(w + "_wk"), g.xn[:, b, :], start=True, stop=True)
                    for t in range(KT):
                        mm = pe.matmul(g.ps[:, 2, t * P:(t + 1) * P], g.xn[:, b, t * P:(t + 1) * P], g.w(w + "_wv"), start=True, stop=True)
                    mm.then_inc(proj, 1)

                def top_scores(u, n):
                    b, i, a = u // 4, u % 4, 17 * u + n
                    if a >= 2:
                        pe.wait_ge(top_in, a - 1)
                    if n == 16:
                        pe.wait_ge(top_in, a)
                        pe.transpose(g.ps[0:16, 4 + a % 2, 0:P], mx[:, u, :], g.w("ident")).then_inc(top, 1)
                        return
                    r, t = n // 4, n % 4
                    mm = pe.matmul(g.ps[:, 4 + a % 2, 0:span(t)], qs[0:ROWS, b, i, r, t * P:(t + 1) * P], ks[0:ROWS, b, i, r, 0:span(t)],
                                   start=True, stop=not causal)
                    if causal:
                        mm = pe.matmul(g.ps[:, 4 + a % 2, t * P:(t + 1) * P], eye, mask_qk, start=False, stop=True)
                    mm.then_inc(top, 1)

                def scores(s):
                    u, kt, half = s // 8, s // 2 % 4, s % 2
                    b, i, q0 = u // 4, u % 4, first(s // 2 % 4)
                    if kt == 0 and half == 0:
                        pe.wait_ge(m_rows, 48 * (u + 1))
                    if s >= 2:
                        pe.wait_ge(prob, s - 1)
                    for x in range(2):
                        r, bank = 2 * half + x, 2 * (s % 2) + x
                        mm = pe.matmul(g.ps[:, bank, q0:T], ks[:, b, i, r, kt * P:(kt + 1) * P], qs[:, b, i, r, q0:T],
                                       start=True, stop=not causal)
                        if causal:
                            mm = pe.matmul(g.ps[:, bank, q0:q0 + P], eye, mask_kq, start=False, stop=True)
                    mm.then_inc(score, 1)

                def products(n):
                    b, i, kt, q0 = n // 16, n // 4 % 4, n % 4, first(n % 4)
                    pe.wait_ge(prob, 2 * n + 2)
                    if n % 16 == 0:
                        pe.wait_ge(vpad_ready, 4)
                        if b >= 1:
                            pe.wait_ge(at_ready, b)
                    begin, end = n % 16 == 0, n % 16 == 15
                    for r in range(4):
                        pe.matmul(g.ps[32 * r:32 * r + 32, 6, q0:T], vpad[:, b, kt, 4 * r + i, :], pt[:, n % 3, r, q0:T],
                                  start=begin, stop=end, skip_group_check=True)
                    for r in range(4):
                        mm = pe.matmul(g.ps[32 * r:32 * r + 32, 7, q0:T], g.w("ones_pad", 32 * i, 32), pt[:, n % 3, r, q0:T],
                                       start=begin, stop=end, skip_group_check=True)
                    mm.then_inc(pv, 1)

                pe.wait_ge(stacked, 16 * 2 * 4 * len(Q_PART) * NB)
                pe.wait_ge(ones_in, 1)
                pe.wait_ge(v_in, NB)
                for u in range(2):
                    for n in range(17):
                        top_scores(u, n)
                for s in range(8 * UN):
                    scores(s)
                    if s % 2 == 0 and s >= 2:
                        products(s // 2 - 1)
                    u = s // 8 + 2
                    if u < UN:
                        for n in range(2 * (s % 8), 2 * (s % 8) + 2):
                            top_scores(u, n)
                        if s % 8 == 7:
                            top_scores(u, 16)
                products(4 * UN - 1)
                for b in range(NB):
                    pe.wait_ge(at_bias, b + 1)
                    pe.matmul(g.ps[:, b, :], g.w(w + "_wo"), at[:, b, :], start=True, stop=True).then_inc(out_ready, 1)

            @block.scalar
            def _(act):
                ln.scalar(act)
                for b in range(NB):
                    act.wait_ge(proj, b + 1)
                    act.activation(v[:, b, :, :], g.ps[:, 2, :].rearrange("p (t c) -> p t c", c=P), ACT.Copy).then_inc(v_in, 1)
                for s in range(8 * UN):
                    n, half, q0 = s // 2, s % 2, first(s // 2 % 4)
                    act.wait_ge(score, s + 1)
                    if n >= 3:
                        act.wait_ge(pv, n - 2)
                    act.activation(pt[:, n % 3, 2 * half:2 * half + 2, q0:T], g.ps[:, 2 * (s % 2):2 * (s % 2) + 2, q0:T], ACT.Exp).then_inc(prob, 1)

            @block.gpsimd
            def _(pool):
                pool.memset(ks[32:ROWS + 3, :, :, :, :], 1.0).then_inc(ones_in, 1)
                pool.wait_ge(ones_in, 1)
                pool.memset(vpad[:, :, :, :, :], 0.0).then_inc(zero, 1)
                pool.wait_ge(zero, 1)
                pool.wait_ge(v_in, NB)
                for c in range(4):
                    for b in range(NB):
                        for t in range(KT):
                            ins = pool.tensor_copy(vpad[:, b, t, c:H:4, 8 * c:8 * c + 8],
                                                   v[:, b, t, :].rearrange("p (r c f) -> p r c f", r=4, c=4)[:, :, c, :])
                    ins.then_inc(vpad_ready, 1)

            @block.vector
            def _(dve):
                ln.vector(dve)
                for b in range(NB):
                    dve.wait_ge(proj, b + 1)
                    if b >= 1:
                        dve.wait_ge(cuts, 5 * b)
                        dve.wait_ge(parted, 16 * b)
                    dve.tensor_scalar(val[:, 0, :], g.ps[:, 0, :], g.w(w + "_bq"), scale, ALU.add, ALU.mult).then_inc(proj_in, 1)
                    dve.tensor_scalar(val[:, 1, :], g.ps[:, 1, :], g.w(w + "_bk"), None, ALU.add).then_inc(proj_in, 1)
                    dve.wait_ge(proj_in, 2 * b + 2)
                    dve.tensor_copy(cut[:, 0, :, :], val[:, :, :]).then_inc(cuts, 1)
                    dve.wait_ge(cuts, 5 * b + 1)
                    dve.tensor_tensor(val[:, :, :], val[:, :, :], cut[:, 0, :, :], ALU.subtract).then_inc(cuts, 1)
                    dve.wait_ge(cuts, 5 * b + 2)
                    dve.tensor_copy(cut[:, 1, :, :], val[:, :, :]).then_inc(cuts, 1)
                    dve.wait_ge(cuts, 5 * b + 3)
                    dve.tensor_tensor(val[:, :, :], val[:, :, :], cut[:, 1, :, :], ALU.subtract).then_inc(cuts, 1)
                    dve.wait_ge(cuts, 5 * b + 4)
                    dve.tensor_copy(cut[:, 2, :, :], val[:, :, :]).then_inc(cuts, 1)

                def maxima(u, n):
                    a = 17 * u + n
                    dve.wait_ge(top, a + 1)
                    if n < 16:
                        dve.tensor_reduce(mx[:, u, n:n + 1], g.ps[:, 4 + a % 2, 0:span(n % 4)], AX.X, ALU.max).then_inc(top_in, 1)
                        return
                    k = 6 * u
                    if u >= 1:
                        dve.wait_ge(m_steps, k)
                    if u >= 2:
                        dve.wait_ge(m_rows, 48 * (u - 1))
                    dve.tensor_scalar(mt[:, 0, :], g.ps[0:16, 4 + a % 2, 0:P], -1.0, None, ALU.mult).then_inc(top_in, 1)
                    dve.wait_ge(top_in, a + 1)
                    dve.tensor_copy(mcut[:, u % 2, 0, :], mt[:, 0, :]).then_inc(m_steps, 1)
                    dve.wait_ge(m_steps, k + 1)
                    dve.tensor_tensor(mt[:, 1, :], mt[:, 0, :], mcut[:, u % 2, 0, :], ALU.subtract).then_inc(m_steps, 1)
                    dve.wait_ge(m_steps, k + 2)
                    dve.tensor_copy(mcut[:, u % 2, 1, :], mt[:, 1, :]).then_inc(m_steps, 1)
                    dve.wait_ge(m_steps, k + 3)
                    dve.tensor_tensor(mt[:, 1, :], mt[:, 1, :], mcut[:, u % 2, 1, :], ALU.subtract).then_inc(m_steps, 1)
                    dve.wait_ge(m_steps, k + 4)
                    dve.tensor_copy(mcut[:, u % 2, 2, :], mt[:, 1, :]).then_inc(m_steps, 2)

                def normalise(b):
                    dve.wait_ge(pv, 16 * (b + 1))
                    dve.reciprocal(inv, g.ps[:, 7, :]).then_inc(inv_ready, 1)
                    dve.wait_ge(inv_ready, b + 1)
                    dve.tensor_tensor(at[:, b, :], g.ps[:, 6, :], inv, ALU.mult).then_inc(at_ready, 1)
                    dve.wait_ge(at_ready, b + 1)
                    dve.tensor_scalar(at[:, b, :], at[:, b, :], g.w(w + "_bv"), None, ALU.add).then_inc(at_bias, 1)

                for u in range(2):
                    for n in range(17):
                        maxima(u, n)
                for u in range(UN):
                    if u + 2 < UN:
                        for n in range(17):
                            maxima(u + 2, n)
                    if u % 4 == 3:
                        normalise(u // 4)
                for b in range(NB):
                    dve.wait_ge(out_ready, b + 1)
                    dve.scalar_tensor_tensor(out=g.xs[:, b, :], in0=g.ps[:, b, :], scalar=g.w(w + "_bo"), in1=g.xs[:, b, :],
                                             op0=ALU.add, op1=ALU.add).then_inc(added, 1)


def wide_attention(g, name):
    PAIRS = H // 2
    UN = NB * PAIRS
    scale = HE ** -0.5
    with Stage(g, name) as st:
        ln = Norm(st, (0, 2), (1, 3))
        q = st.sb("q", [HE + 1, 3, 2, T])
        k = st.sb("k", [HE + 1, 3, 2, T])
        v = st.sb("v", [P, 3, 2, KT, P])
        pt = st.sb("pt", [P, 3, T])
        mx = st.sb("mx", [P, 2, 8])
        mt = st.sb("mt", [8, 2, P])
        inv = st.sb("inv", [P, 2, T])
        at = st.sb("at", [P, NB, PAIRS, T])
        ones_in, proj, proj_in = st.sem("ones_in"), st.sem("proj"), st.sem("proj_in")
        top, top_in, m_rows, score, prob, pv = (st.sem(n) for n in ("top", "top_in", "m_rows", "score", "prob", "pv"))
        inv_ready, at_ready, out_ready, added = (st.sem(n) for n in ("inv_ready", "at_ready", "out_ready", "added"))
        with g.nc.Block() as block:
            @block.sync
            def _(sp):
                st.clear_spent(sp)
                for u in range(UN):
                    sp.wait_ge(top_in, 9 * u + 9)
                    sp.dma_start(q[HE:HE + 1, u % 3, :, :].rearrange("o h (t c) -> o (h t) c", c=P), mt[:, u % 2, :]).then_inc(m_rows, 16)
                    sp.wait_ge(m_rows, 16 * (u + 1))

            @block.tensor
            def _(pe):
                ln.tensor(pe)

                def project(u):
                    b, p = u // PAIRS, u % PAIRS
                    for j in range(3):
                        n = 3 * u + j
                        if n >= 2:
                            pe.wait_ge(proj_in, 2 * (n - 1))
                        if j < 2:
                            pe.matmul(g.ps[:, n % 2, :], g.w("w1_w" + "qk"[j], p * P, P), g.xn[:, b, :], start=True, stop=True).then_inc(proj, 1)
                            continue
                        for t in range(KT):
                            mm = pe.matmul(g.ps[:, n % 2, t * P:(t + 1) * P], g.xn[:, b, t * P:(t + 1) * P], g.w("w1_wv", p * P, P),
                                           start=True, stop=True)
                        mm.then_inc(proj, 1)

                def top_scores(u, n):
                    a = 9 * u + n
                    if a >= 2:
                        pe.wait_ge(top_in, a - 1)
                    if n == 8:
                        pe.wait_ge(top_in, a)
                        pe.transpose(g.ps[0:8, 2 + a % 2, 0:P], mx[:, u % 2, :], g.w("ident")).then_inc(top, 1)
                        return
                    if n == 0:
                        pe.wait_ge(proj_in, 6 * u + 4)
                    h, t = n // 4, n % 4
                    pe.matmul(g.ps[:, 2 + a % 2, :], q[0:HE, u % 3, h, t * P:(t + 1) * P], k[0:HE, u % 3, h, :], start=True, stop=True).then_inc(top, 1)

                def scores(s):
                    u, h, t = s // 8, s // 4 % 2, s % 4
                    if s % 8 == 0:
                        pe.wait_ge(m_rows, 16 * (u + 1))
                    if s >= 2:
                        pe.wait_ge(prob, s - 1)
                    pe.matmul(g.ps[:, 4 + s % 2, :], k[:, u % 3, h, t * P:(t + 1) * P], q[:, u % 3, h, :], start=True, stop=True).then_inc(score, 1)

                def products(s):
                    u, h, t = s // 8, s // 4 % 2, s % 4
                    pe.wait_ge(prob, s + 1)
                    if t == 0:
                        pe.wait_ge(proj_in, 6 * u + 6)
                        if u >= 1:
                            pe.wait_ge(at_ready, 2 * u - 1 + h)
                    pe.matmul(g.ps[:, 6 + h, :], v[:, u % 3, h, t, :], pt[:, s % 3, :], start=(t == 0), stop=(t == KT - 1)).then_inc(pv, 1)

                pe.wait_ge(ln.done, NB)
                pe.wait_ge(ones_in, 2)
                project(0)
                project(1)
                for n in range(9):
                    top_scores(0, n)
                for s in range(8 * UN):
                    u = s // 8
                    scores(s)
                    if s >= 1:
                        products(s - 1)
                    if u + 1 < UN:
                        top_scores(u + 1, s % 8)
                        if s % 8 == 7:
                            top_scores(u + 1, 8)
                    if s % 8 == 7 and u + 2 < UN:
                        project(u + 2)
                products(8 * UN - 1)
                for b in range(NB):
                    pe.wait_ge(at_ready, 2 * PAIRS * (b + 1))
                    for p in range(PAIRS):
                        mm = pe.matmul(g.ps[:, b, :], g.w("w1_wp", p * P, P), at[:, b, p, :], start=(p == 0), stop=(p == PAIRS - 1))
                    mm.then_inc(out_ready, 1)

            @block.scalar
            def _(act):
                ln.scalar(act)

                def take(u):
                    for j in range(3):
                        n = 3 * u + j
                        act.wait_ge(proj, n + 1)
                        if j == 0 and u >= 3:
                            act.wait_ge(pv, 8 * (u - 2))
                        for h in range(2):
                            src = g.ps[HE * h:HE * h + HE, n % 2, :]
                            if j == 0:
                                ins = act.activation(q[0:HE, u % 3, h, :], src, ACT.Copy, scale=scale)
                            elif j == 1:
                                ins = act.activation(k[0:HE, u % 3, h, :], src, ACT.Copy)
                            else:
                                ins = act.activation(v[:, u % 3, h, :, HE * h:HE * h + HE],
                                                     g.ps[:, n % 2, :].rearrange("p (t c) -> p t c", c=P)[:, :, HE * h:HE * h + HE], ACT.Copy)
                            ins.then_inc(proj_in, 1)

                act.wait_ge(ones_in, 2)
                take(0)
                take(1)
                for s in range(8 * UN):
                    act.wait_ge(score, s + 1)
                    if s >= 3:
                        act.wait_ge(pv, s - 2)
                    act.activation(pt[:, s % 3, :], g.ps[:, 4 + s % 2, :], ACT.Exp).then_inc(prob, 1)
                    if s % 8 == 7 and s // 8 + 2 < UN:
                        take(s // 8 + 2)

            @block.gpsimd
            def _(pool):
                pool.memset(v[:, :, :, :, :], 1.0).then_inc(ones_in, 1)
                pool.wait_ge(ones_in, 1)
                pool.memset(k[HE:HE + 1, :, :, :], 1.0).then_inc(ones_in, 1)

            @block.vector
            def _(dve):
                ln.vector(dve)

                def maxima(u, n):
                    a = 9 * u + n
                    dve.wait_ge(top, a + 1)
                    if n < 8:
                        dve.tensor_reduce(mx[:, u % 2, n:n + 1], g.ps[:, 2 + a % 2, :], AX.X, ALU.max).then_inc(top_in, 1)
                        return
                    if u >= 2:
                        dve.wait_ge(m_rows, 16 * (u - 1))
                    dve.tensor_scalar(mt[:, u % 2, :], g.ps[0:8, 2 + a % 2, 0:P], -1.0, None, ALU.mult).then_inc(top_in, 1)

                def normalise(u, h):
                    b, p = u // PAIRS, u % PAIRS
                    mine, other = slice(HE * h, HE * h + HE), slice(HE - HE * h, P - HE * h)
                    dve.wait_ge(pv, 8 * u + 4 * h + 4)
                    if u >= 1:
                        dve.wait_ge(at_ready, 2 * u - 1 + h)
                    dve.reciprocal(inv[mine, h, :], g.ps[other, 6 + h, :]).then_inc(inv_ready, 1)
                    dve.wait_ge(inv_ready, 2 * u + h + 1)
                    dve.tensor_tensor(at[mine, b, p, :], g.ps[mine, 6 + h, :], inv[mine, h, :], ALU.mult).then_inc(at_ready, 1)

                for n in range(9):
                    maxima(0, n)
                for u in range(UN):
                    for n in range(5):
                        if u + 1 < UN:
                            maxima(u + 1, n)
                    normalise(u, 0)
                    for n in range(5, 9):
                        if u + 1 < UN:
                            maxima(u + 1, n)
                    normalise(u, 1)
                for b in range(NB):
                    dve.wait_ge(out_ready, b + 1)
                    dve.scalar_tensor_tensor(out=g.xs[:, b, :], in0=g.ps[:, b, :], scalar=g.w("w1_bp"), in1=g.xs[:, b, :],
                                             op0=ALU.add, op1=ALU.add).then_inc(added, 1)


def relu_attention(g, name):
    UN = NB * 4
    R = 96
    with Stage(g, name) as st:
        ln = Norm(st, (0, 1), (2, 3))
        qk = st.sb("qk", [P, 2, 2, KT, P])
        rows = st.sb("rows", [P, 2, KT, P])
        rt = st.sb("rt", [P, 2, T])
        hid = st.sb("hid", [P, 2 * NB, T])
        z = st.sb("z", [R, 2 * NB, T])
        sums = st.sb("sums", [R, 2 * NB, 2])
        std = st.sb("std", [R, NB])
        cut = st.sb("cut", [R, T], BF16)
        zc = st.sb("zc", [R, 2, NB, T], BF16)
        zk = st.sb("zk", [P, NB, KT, H])
        v = st.sb("v", [P, NB, KT, P])
        vpad = st.sb("vpad", [P, NB, KT, H, 32])
        qb = st.sb("qb", [P, 2, 4, T])
        re = st.sb("re", [P, 3, 4, T])
        proj, qk_in, v_in, mean_v, centred_v, zero, vpad_ready = (
            st.sem(n) for n in ("proj", "qk_in", "v_in", "mean_v", "centred_v", "zero", "vpad_ready"))
        sent, rows_in, turned, turned_in, hidden, hid_in, zraw = (
            st.sem(n) for n in ("sent", "rows_in", "turned", "turned_in", "hidden", "hid_in", "zraw"))
        z_in, z_c, z_sq, z_var, z_log, z_std, z_ready, cuts, zk_turned, zk_in = (
            st.sem(n) for n in ("z_in", "z_c", "z_sq", "z_var", "z_log", "z_std", "z_ready", "cuts", "zk_turned", "zk_in"))
        spread_q, qb_in, relu_dve, relu_act, pv, norm_row, norm, done, added = (
            st.sem(n) for n in ("spread_q", "qb_in", "relu_dve", "relu_act", "pv", "norm_row", "norm", "done", "added"))
        row_steps, cut_rest, norm_steps = st.sem("row_steps"), st.sem("cut_rest"), st.sem("norm_steps")
        with g.nc.Block() as block:
            @block.sync
            def _(sp):
                st.clear_spent(sp)
                for x in range(2 * NB):
                    b, j = x // 2, x % 2
                    sp.wait_ge(qk_in, x + 1)
                    sp.dma_start(g.rows_dram[x].rearrange("(t p) c -> p t c", p=P), qk[:, b, j, :, :]).then_inc(sent, 16)
                    sp.wait_ge(sent, 16 * (x + 1))
                    if x >= 2:
                        sp.wait_ge(turned, x - 1)
                    for h in range(H):
                        src = g.rows_dram[x].rearrange("(n s) (h f) -> h n s f", s=16, f=DH)[h]
                        sp.dma_start(rows[32 * (h % 4):32 * (h % 4) + 32, x % 2, h // 4, :].rearrange("p (s f) -> p s f", f=DH), src).then_inc(rows_in, 16)
                    sp.wait_ge(rows_in, 16 * H * (x + 1))

            @block.tensor
            def _(pe):
                ln.tensor(pe)
                pe.wait_ge(ln.done, NB)
                for b in range(NB):
                    for j, wt in enumerate(("r3_wq", "r3_wk", "r3_wv")):
                        n = 3 * b + j
                        if n == 2:
                            pe.wait_ge(qk_in, 1)
                        elif n == 3:
                            pe.wait_ge(qk_in, 2)
                        elif n == 4:
                            pe.wait_ge(v_in, 1)
                        elif n == 5:
                            pe.wait_ge(qk_in, 3)
                        for t in range(KT):
                            mm = pe.matmul(g.ps[:, 4 + n % 2, t * P:(t + 1) * P], g.xn[:, b, t * P:(t + 1) * P], g.w(wt), start=True, stop=True)
                        mm.then_inc(proj, 1)
                for b in range(NB):
                    pe.wait_ge(v_in, b + 1)
                    for t in range(KT):
                        mm = pe.matmul(g.ps[:, 6 + b, 0:P], g.w("mean_mat"), v[:, b, t, :], start=(t == 0), stop=(t == KT - 1))
                    mm.then_inc(mean_v, 1)
                for x in range(2 * NB):
                    pe.wait_ge(rows_in, 16 * H * (x + 1))
                    if x >= 2:
                        pe.wait_ge(turned_in, x - 1)
                    for t in range(KT):
                        mm = pe.transpose(g.ps[:, x % 2, t * P:(t + 1) * P], rows[:, x % 2, t, :], g.w("ident"))
                    mm.then_inc(turned, 1)
                    pe.wait_ge(turned_in, x + 1)
                    if x >= 2:
                        pe.wait_ge(hid_in, x - 1)
                    pe.matmul(g.ps[:, 2 + x % 2, :], g.w("r3_w1"), rt[:, x % 2, :], start=True, stop=True).then_inc(hidden, 1)
                for x in range(2 * NB):
                    pe.wait_ge(hid_in, x + 1)
                    if x >= 2:
                        pe.wait_ge(z_in, x - 1)
                    if x == 0:
                        pe.wait_ge(qk_in, 2 * NB)
                        pe.wait_ge(v_in, NB)
                    pe.matmul(g.ps[0:R, 4 + x % 2, :], g.w("r3_w2"), hid[:, x, :], start=True, stop=True).then_inc(zraw, 1)
                for b in range(NB):
                    pe.wait_ge(z_ready, 2 * b + 2)
                    pe.wait_ge(turned_in, 2 * NB)
                    for t in range(KT):
                        mm = pe.transpose(g.ps[:, b, t * H:(t + 1) * H], z[0:H, 2 * b + 1, t * P:(t + 1) * P], g.w("ident")[0:H, 0:H])
                    mm.then_inc(zk_turned, 1)

                def spread(u):
                    b, i = u // 4, u % 4
                    if u >= 1:
                        pe.wait_ge(qb_in, u)
                    for r in range(4):
                        mm = pe.matmul(g.ps[:, r, :], widen(g.cb[0:R, 384 + 4 * r + i:385 + 4 * r + i], P), zc[:, 0, b, :], start=True, stop=True)
                    mm.then_inc(spread_q, 1)

                pe.wait_ge(cuts, 10 * NB)
                pe.wait_ge(zk_in, NB)
                pe.wait_ge(hid_in, 2 * NB)
                pe.wait_ge(vpad_ready, 4)
                spread(0)
                for n in range(4 * UN):
                    b, i, t = n // 16, n // 4 % 4, n % 4
                    if t == 0 and n // 4 + 1 < UN:
                        spread(n // 4 + 1)
                    if t == 3:
                        pe.wait_ge(relu_act, 4 * (n // 4 + 1))
                    else:
                        pe.wait_ge(relu_dve, 4 * (3 * (n // 4) + t + 1))
                    if n % 16 == 0 and b >= 1:
                        pe.wait_ge(norm, b)
                        pe.wait_ge(done, b)
                    begin, end = n % 16 == 0, n % 16 == 15
                    for r in range(4):
                        pe.matmul(g.ps[32 * r:32 * r + 32, 6, :], vpad[:, b, t, 4 * r + i, :], re[:, n % 3, r, :], start=begin, stop=end, skip_group_check=True)
                    for r in range(4):
                        mm = pe.matmul(g.ps[32 * r:32 * r + 32, 7, :], g.w("ones_pad", 32 * i, 32), re[:, n % 3, r, :], start=begin, stop=end, skip_group_check=True)
                    mm.then_inc(pv, 1)
                    if n % 16 == 15:
                        pe.matmul(g.ps[:, 5, :], g.cb[0:R, 416:416 + P], zc[:, 1, b, :], start=True, stop=True).then_inc(norm_row, 1)

            @block.scalar
            def _(act):
                ln.scalar(act)
                for x in range(2 * NB):
                    act.wait_ge(turned, x + 1)
                    if x >= 2:
                        act.wait_ge(hidden, x - 1)
                    act.activation(rt[:, x % 2, :], g.ps[:, x % 2, :], ACT.Copy).then_inc(turned_in, 1)
                    act.wait_ge(hidden, x + 1)
                    act.activation(hid[:, x, :], g.ps[:, 2 + x % 2, :], ACT.Gelu, bias=g.w("r3_b1")).then_inc(hid_in, 1)
                for x in range(2 * NB):
                    act.wait_ge(zraw, x + 1)
                    act.activation(z[:, x, :], g.ps[0:R, 4 + x % 2, :], ACT.Identity, bias=g.w("r3_b2"), accum_out=sums[:, x, 0:1]).then_inc(z_in, 1)
                for x in range(2 * NB):
                    act.wait_ge(z_c, 2 * x + 2)
                    act.activation(qb[0:R, 0, x, :], z[:, x, :], ACT.Square, accum_out=sums[:, x, 1:2]).then_inc(z_sq, 1)
                for b in range(NB):
                    act.wait_ge(z_var, b + 1)
                    act.activation(std[:, b:b + 1], std[:, b:b + 1], ACT.Ln, scale=0.5 / T, bias=g.w("eps6")[0:R, :]).then_inc(z_log, 1)
                    act.wait_ge(z_log, b + 1)
                    act.activation(std[:, b:b + 1], std[:, b:b + 1], ACT.Exp, scale=-0.5).then_inc(z_std, 1)
                for b in range(NB):
                    act.wait_ge(zk_turned, b + 1)
                    act.activation(zk[:, b, :, :], g.ps[:, b, 0:KT * H].rearrange("p (t h) -> p t h", h=H), ACT.Copy, scale=-1.0).then_inc(zk_in, 1)
                act.wait_ge(zk_in, NB)
                for u in range(UN):
                    b, i = u // 4, u % 4
                    act.wait_ge(spread_q, u + 1)
                    if u >= 2:
                        act.wait_ge(relu_dve, 12 * (u - 1))
                        act.wait_ge(relu_act, 4 * (u - 1))
                    act.activation(qb[:, u % 2, :, :], g.ps[:, 0:4, :], ACT.Copy).then_inc(qb_in, 1)
                    act.wait_ge(qb_in, u + 1)
                    n = 4 * u + 3
                    act.wait_ge(pv, n - 2)
                    for r in range(4):
                        act.activation(re[:, n % 3, r, :], qb[:, u % 2, r, :], ACT.Relu, bias=zk[:, b, 3, 4 * r + i:4 * r + i + 1]).then_inc(relu_act, 1)

            @block.gpsimd
            def _(pool):
                pool.memset(vpad[:, :, :, :, :], 0.0).then_inc(zero, 1)
                pool.wait_ge(zero, 1)
                pool.wait_ge(centred_v, NB)
                for c in range(4):
                    for b in range(NB):
                        for t in range(KT):
                            ins = pool.tensor_copy(vpad[:, b, t, c:H:4, 8 * c:8 * c + 8],
                                                   v[:, b, t, :].rearrange("p (r c f) -> p r c f", r=4, c=4)[:, :, c, :])
                    ins.then_inc(vpad_ready, 1)

            @block.vector
            def _(dve):
                ln.vector(dve)
                for b in range(NB):
                    for j, bias in enumerate(("r3_bq_row", "r3_bk_row")):
                        n = 3 * b + j
                        dve.wait_ge(proj, n + 1)
                        dve.tensor_tensor(qk[:, b, j, :, :], g.ps[:, 4 + n % 2, :].rearrange("p (t c) -> p t c", c=P),
                                          bcast(g.w(bias), 1, KT), ALU.add).then_inc(qk_in, 1)
                    n = 3 * b + 2
                    dve.wait_ge(proj, n + 1)
                    dve.tensor_copy(v[:, b, :, :], g.ps[:, 4 + n % 2, :].rearrange("p (t c) -> p t c", c=P)).then_inc(v_in, 1)
                for b in range(NB):
                    dve.wait_ge(mean_v, b + 1)
                    dve.scalar_tensor_tensor(out=v[:, b, :, :], in0=bcast(g.ps[:, 6 + b, 0:P], 1, KT), scalar=-1.0 / KT, in1=v[:, b, :, :],
                                             op0=ALU.mult, op1=ALU.add).then_inc(centred_v, 1)
                for x in range(2 * NB):
                    dve.wait_ge(z_in, x + 1)
                    dve.tensor_scalar(sums[:, x, 0:1], sums[:, x, 0:1], 1.0 / T, None, ALU.mult).then_inc(z_c, 1)
                    dve.wait_ge(z_c, 2 * x + 1)
                    dve.tensor_scalar(z[:, x, :], z[:, x, :], sums[:, x, 0:1], None, ALU.subtract).then_inc(z_c, 1)
                for b in range(NB):
                    dve.wait_ge(z_sq, 2 * b + 2)
                    dve.tensor_tensor(std[:, b:b + 1], sums[:, 2 * b, 1:2], sums[:, 2 * b + 1, 1:2], ALU.add).then_inc(z_var, 1)
                for b in range(NB):
                    dve.wait_ge(z_std, b + 1)
                    for x in (2 * b, 2 * b + 1):
                        dve.tensor_scalar(z[:, x, :], z[:, x, :], std[:, b:b + 1], None, ALU.mult).then_inc(z_ready, 1)
                    dve.wait_ge(z_ready, 2 * b + 2)
                    dve.tensor_reduce(sums[:, 2 * b + 1, 0:1], z[:, 2 * b + 1, :], AX.X, ALU.add).then_inc(row_steps, 1)
                    dve.wait_ge(row_steps, 2 * b + 1)
                    dve.tensor_scalar(qb[0:R, 1, b, :], z[:, 2 * b, :], float(T), sums[:, 2 * b + 1, 0:1], ALU.mult, ALU.subtract).then_inc(row_steps, 1)
                    dve.wait_ge(row_steps, 2 * b + 2)
                    for j in range(2):
                        src = (z[:, 2 * b, :], qb[0:R, 1, b, :])[j]
                        rest = qb[0:R, 0, j, :]
                        k = 10 * b + 5 * j
                        if b or j:
                            dve.wait_ge(cuts, k)
                        dve.wait_ge(z_sq, 2 * NB)
                        dve.tensor_copy(zc[0:32, j, b, :], src[0:32, :]).then_inc(cuts, 1)
                        dve.tensor_copy(cut[:, :], src).then_inc(cuts, 1)
                        dve.wait_ge(cuts, k + 2)
                        dve.tensor_tensor(rest, src, cut[:, :], ALU.subtract).then_inc(cut_rest, 1)
                        dve.wait_ge(cut_rest, 4 * b + 2 * j + 1)
                        dve.tensor_copy(zc[32:64, j, b, :], rest[32:64, :]).then_inc(cuts, 1)
                        dve.tensor_copy(cut[:, :], rest).then_inc(cuts, 1)
                        dve.wait_ge(cuts, k + 4)
                        dve.tensor_tensor(rest, rest, cut[:, :], ALU.subtract).then_inc(cut_rest, 1)
                        dve.wait_ge(cut_rest, 4 * b + 2 * j + 2)
                        dve.tensor_copy(zc[64:96, j, b, :], rest[64:96, :]).then_inc(cuts, 1)
                dve.wait_ge(zk_in, NB)
                for u in range(UN):
                    b, i = u // 4, u % 4
                    dve.wait_ge(qb_in, u + 1)
                    for t in range(3):
                        n = 4 * u + t
                        if n >= 3:
                            dve.wait_ge(pv, n - 2)
                        for r in range(4):
                            dve.tensor_scalar(re[:, n % 3, r, :], qb[:, u % 2, r, :], zk[:, b, t, 4 * r + i:4 * r + i + 1], 0.0,
                                              ALU.add, ALU.max).then_inc(relu_dve, 1)
                    if i == 3:
                        dve.wait_ge(norm_row, b + 1)
                        dve.wait_ge(pv, 16 * (b + 1))
                        if b >= 1:
                            dve.wait_ge(added, b)
                        dve.tensor_scalar(ln.xc[:, 0, :], g.ps[:, 7, :], 2.0, None, ALU.mult).then_inc(norm_steps, 1)
                        dve.wait_ge(norm_steps, 3 * b + 1)
                        dve.tensor_tensor(ln.xc[:, 0, :], ln.xc[:, 0, :], g.ps[:, 5, :], ALU.subtract).then_inc(norm_steps, 1)
                        dve.wait_ge(norm_steps, 3 * b + 2)
                        dve.tensor_scalar(ln.xc[:, 0, :], ln.xc[:, 0, :], 1e-4, None, ALU.max).then_inc(norm_steps, 1)
                        dve.wait_ge(norm_steps, 3 * b + 3)
                        dve.reciprocal(ln.xc[:, 1, :], ln.xc[:, 0, :]).then_inc(norm, 1)
                        dve.wait_ge(norm, b + 1)
                        dve.scalar_tensor_tensor(out=ln.sq[:, b, :], in0=g.ps[:, 6, :], scalar=2.0, in1=ln.xc[:, 1, :],
                                                 op0=ALU.mult, op1=ALU.mult).then_inc(done, 1)
                        dve.wait_ge(done, b + 1)
                        dve.tensor_tensor(g.xs[:, b, :], g.xs[:, b, :], ln.sq[:, b, :], ALU.add).then_inc(added, 1)
def network(nc, x_dram, wd, experts, boold, intd, out_dram, cols):
    ctx = ExitStack()
    with ctx:
        g = Net(nc, ctx, cols)

        def sb(name, shape, dt=F32):
            return ctx.enter_context(nc.sbuf_tensor(name, shape, dt))

        g.weights = sb("weights", [P, wd.shape[1]])
        g.tern = sb("tern", [P, P])
        g.conn = sb("conn", [P, boold.shape[1] - FF])
        g.gated = sb("gated", [P, intd.shape[1]])
        g.s2x = sb("s2x", [P, 2])
        g.A = sb("A", [P, 2, 2 * NS])
        g.cb = sb("cb", [P, cols["bf_consts"][2]], BF16)
        g.xs = sb("xs", [P, NB, T])
        g.xn = sb("xn", [P, NB, T])
        g.ps = ctx.enter_context(nc.psum_tensor("ps", [P, 8, T], F32))

        g.experts = experts
        g.parts_dram = nc.dram_tensor("parts_dram", [NB, P, 3, 2, T], BF16, kind="Internal").ap()
        g.rows_dram = nc.dram_tensor("rows_dram", [2 * NB, T, P], F32, kind="Internal").ap()
        g.stored = ctx.enter_context(nc.semaphore("stored"))

        prepare(g, wd, boold, intd)
        with nc.Fori(0, BATCH // NB, 1) as i:
            load_x(g, x_dram, i)
            layers = [
                lambda: mamba(g, "L0a", "m0", 0),
                lambda: ternary_ffn(g, "L0f"),
                lambda: narrow_attention(g, "L0b", "a0", False, 19.5 / 128.0),
                lambda: ternary_ffn(g, "L0g"),
                lambda: linear_attention(g, "L1a"),
                lambda: connection_ffn(g, "L1f"),
                lambda: wide_attention(g, "L1b"),
                lambda: connection_ffn(g, "L1g"),
                lambda: single_head_attention(g, "L2a"),
                lambda: expert_ffn(g, "L2f"),
                lambda: narrow_attention(g, "L2b", "a2", True, DH ** -0.5),
                lambda: expert_ffn(g, "L2g"),
                lambda: mamba(g, "L3a", "m3", 1),
                lambda: gated_ffn(g, "L3f"),
                lambda: relu_attention(g, "L3b"),
                lambda: gated_ffn(g, "L3g"),
            ]
            for k in STAGES:
                layers[k]()
            store_x(g, out_dram, i)
        g.spent_ctx.close()


STAGES = range(16)


def _pack(inp):
    import numpy as np
    f = np.float32
    parts = []

    def put(name, a):
        parts.append((name, np.asarray(a)))

    def col(v):
        return np.asarray(v).reshape(-1, 128).T

    def tiles(m):
        m = np.asarray(m)
        return m.reshape(-1, 128, m.shape[1]).transpose(1, 0, 2).reshape(128, -1)

    def over(v, n=128):
        v = np.asarray(v).reshape(1, -1)
        return np.broadcast_to(v, (n, v.shape[1]))

    eye = np.eye(128, dtype=f)
    r = np.arange(128)
    put("mean_mat", np.full((128, 128), 1 / 128, f))
    put("ident", eye)
    put("eps5", np.full((128, 1), 1e-5, f))
    put("eps6", np.full((128, 1), 1e-6, f))
    put("head_sum", (r[:, None] // 8 == r[None, :] // 8).astype(f))
    put("head_cum", ((r[:, None] % 8 == r[None, :] % 8) & (r[:, None] // 8 <= r[None, :] // 8)).astype(f))
    put("tri_t", (r[:, None] <= r[None, :]).astype(f))
    put("tri", (r[None, :] <= r[:, None]).astype(f))
    put("rank", over(np.arange(8, 0, -1).astype(f)))
    put("ones_pad", over((np.arange(32)[None, :] // 8 == np.arange(4)[:, None]).astype(f)))
    j = np.arange(32)
    put("head_of", (r[:, None] // 8 % 4 == j[None, :4]).astype(f))
    put("bf_consts", np.concatenate([
        eye,
        np.where(r[None, :] > r[:, None], f(-1e30), f(0)),
        np.where(r[:, None] > r[None, :], f(-1e30), f(0)),
        (r[:, None] % 32 == j[None, :]).astype(f),
        (r[:, None] % 32 == r[None, :] // 8).astype(f),
        np.ones((128, 128), f)], 1))

    def mamba(p, q, in_w, conv_w, conv_b, xp, rank, dtw, dtb, alog, d, out_w):
        put(p + "_in", in_w)
        put(p + "_cw", np.asarray(conv_w).reshape(2, 128, 4).transpose(1, 0, 2).reshape(128, 8))
        put(p + "_cb", col(conv_b))
        xp = np.asarray(xp)
        bc, dt = xp[:, rank:], xp[:, :rank]
        put(p + "_xp", tiles(np.concatenate([bc, bc, bc, dt], 1)))
        m = np.zeros((128, 256), f)
        m[96:96 + rank] = dtw
        put(p + "_dtw", m)
        put(p + "_dtb", col(dtb))
        put(p + "_alog", np.asarray(alog).reshape(2, 128, 16).transpose(1, 0, 2).reshape(128, 32))
        put(p + "_d", col(d))
        put(p + "_out", tiles(out_w))

    a = lambda n: np.asarray(inp[n])
    mamba("m0", "", a("L0_attn_a_in_proj_w").T, a("L0_attn_a_conv_w"), a("L0_attn_a_conv_b"), a("L0_attn_a_x_proj_w").T, 8,
          a("L0_attn_a_dt_proj_w").T, a("L0_attn_a_dt_proj_b"), a("L0_attn_a_A_log"), a("L0_attn_a_D_skip"), a("L0_attn_a_out_proj_w").T)
    put("m0_rms1", col(a("L0_attn_a_rms1_w")))
    put("m0_rms2", col(a("L0_attn_a_rms2_w")))
    put("m0_fc1", a("L0_attn_a_fc1_w").T)
    put("m0_fc1b", col(a("L0_attn_a_fc1_b")))
    put("m0_fc2", tiles(a("L0_attn_a_fc2_w").T))
    put("m0_fc2b", col(a("L0_attn_a_fc2_b")))
    put("m0_fc3", tiles(a("L0_attn_a_fc3_w").T))
    put("m0_fc3b", col(a("L0_attn_a_fc3_b")))
    mamba("m3", "", a("L3_attn_a_W_in"), a("L3_attn_a_conv_w"), a("L3_attn_a_conv_b"), a("L3_attn_a_x_proj_w"), 1,
          a("L3_attn_a_dt_w").reshape(1, 256), a("L3_attn_a_dt_b"), a("L3_attn_a_A_log"), a("L3_attn_a_D"), a("L3_attn_a_W_out"))
    put("m3_nw", col(a("L3_attn_a_norm_w")))
    put("m3_nb", col(a("L3_attn_a_norm_b")))
    put("f0_w", a("L0_ffn_weight").T)
    put("f0_alpha", over(a("L0_ffn_alpha")))
    put("f0_b", col(a("L0_ffn_bias")))
    for p, q in (("a0", "L0_attn_b"), ("a2", "L2_attn_b")):
        for n in "qkvo":
            put(f"{p}_w{n}", a(f"{q}_W{n}").T)
            put(f"{p}_b{n}", col(a(f"{q}_b{n}")))
    for n in "qkvo":
        put(f"l1_w{n}", a(f"L1_attn_a_W{n}"))
    put("l1_bo", col(a("L1_attn_a_bo")))
    put("f1_s", over(np.stack([a("L1_ffn_s0"), a("L1_ffn_s1"), a("L1_ffn_s2")])))
    for n in "qkv":
        put(f"w1_w{n}", a(f"L1_attn_b_W{n}").transpose(1, 0, 2).reshape(128, 1024))
    put("w1_wp", a("L1_attn_b_Wp").reshape(64, 8, 2, 128).transpose(2, 0, 1, 3).reshape(128, 1024))
    put("w1_bp", col(a("L1_attn_b_bp")))
    for n in "QKV":
        put(f"s2_w{n.lower()}", a(f"L2_attn_a_W{n}").T)
    put("e2_gw", a("L2_ffn_gate_w"))
    put("e2_gb", over(a("L2_ffn_gate_b")))
    put("e2_b1", a("L2_ffn_b1").reshape(8, 4, 128).transpose(2, 0, 1).reshape(128, 32))
    experts = np.stack([a("L2_ffn_w1").transpose(1, 0, 2).reshape(128, 4096),
                        a("L2_ffn_w2").reshape(8, 4, 128, 128).transpose(2, 0, 1, 3).reshape(128, 4096)])
    put("e2_b2", a("L2_ffn_b2").T)
    for n in ("Wq", "Wk", "Wv", "W1"):
        put(f"r3_{n.lower()}", a(f"L3_attn_b_{n}"))
    put("r3_bq_row", over(a("L3_attn_b_bq")))
    put("r3_bk_row", over(a("L3_attn_b_bk")))
    put("r3_bv", col(a("L3_attn_b_bv")))
    put("r3_b1", col(a("L3_attn_b_b1")))
    w2, b2 = np.zeros((128, 3, 32), f), np.zeros((3, 32), f)
    w2[:, :, :16], b2[:, :16] = a("L3_attn_b_W2")[:, None, :], a("L3_attn_b_b2")
    put("r3_w2", w2.reshape(128, 96))
    put("r3_b2", b2.reshape(96, 1))
    cols, at = {}, 0
    for name, m in parts:
        cols[name] = (m.shape[0], at, m.shape[1])
        at += m.shape[1]
    blob = np.zeros((128, at), f)
    for name, m in parts:
        blob[:m.shape[0], cols[name][1]:cols[name][1] + m.shape[1]] = m
    k0, k1, k2 = (a(f"L1_ffn_k{n}") for n in range(3))
    bools = np.concatenate([k0[:128], k0[128:], tiles(k1), tiles(k2)], 1)
    ints = np.concatenate([a("L3_ffn_w_gate").T, a("L3_ffn_w_up").T, tiles(a("L3_ffn_w_down").T)], 1)
    return np.ascontiguousarray(blob), cols, experts, np.ascontiguousarray(bools), np.ascontiguousarray(ints)


def kernel(**inputs):
    import numpy as np
    import concourse.bacc as bacc
    from concourse.bass_utils import run_bass_kernel_spmd as run

    nc = bacc.Bacc("TRN2", target_bir_lowering=False, num_devices=1)
    blob, cols, experts, bools, ints = _pack(inputs)
    x = np.ascontiguousarray(np.asarray(inputs["L0_attn_a_x"]).transpose(0, 2, 1))
    arrays = {"x_dram": x, "w_dram": blob, "expert_dram": experts, "bool_dram": bools, "int_dram": ints}
    aps = {n: nc.dram_tensor(n, v.shape, mybir.dt.from_np(v.dtype), kind="ExternalInput").ap() for n, v in arrays.items()}
    out = nc.dram_tensor("out_dram", x.shape, F32, kind="ExternalOutput").ap()
    network(nc, aps["x_dram"], aps["w_dram"], aps["expert_dram"], aps["bool_dram"], aps["int_dram"], out, cols)
    r = run(nc, [arrays], core_ids=[0])
    return np.ascontiguousarray(r.results[0]["out_dram"].transpose(0, 2, 1))
```
